# Optimizing a Trainium2 kernel written in Bass

```python
import numpy as np
import jax
import jax.numpy as jnp

def _softmax(x, axis=-1):
    return jax.nn.softmax(x, axis=axis)

def _gelu(x):
    return jax.nn.gelu(x, approximate=True)

def _silu(x):
    return jax.nn.silu(x)

def _sigmoid(x):
    return jax.nn.sigmoid(x)

def _layernorm(x, axis=-1, eps=1e-05):
    m = jnp.mean(x, axis=axis, keepdims=True)
    v = jnp.var(x, axis=axis, keepdims=True)
    return (x - m) / jnp.sqrt(v + eps)

def _scatter_add(tgt, idx, src, axis=0):
    return tgt.at[idx].add(src)

def _segment_sum(src, seg, n):
    return jax.ops.segment_sum(src, seg, n)
kernel_name = 'mk_seq_preln_d1_jaxref_r4_122d7d'

def setup_inputs(seed: int=0):
    np.random.seed(seed)
    _w = jnp.asarray

    def _L0_attn_setup():
        import jax, jax.numpy as jnp
        import numpy as np
        import math
        D_MODEL = 512
        NUM_HEADS = 16
        D_K = D_MODEL // NUM_HEADS
        SEQ_LEN = 512
        THETA = 10000.0
        BATCH = 2

        def _rope(t):
            S = t.shape[-2]
            dk = t.shape[-1]
            inv_freq = jnp.exp(-math.log(THETA) * jnp.arange(0, dk, 2, dtype=jnp.float32) / dk)
            pos = jnp.arange(S, dtype=jnp.float32)
            freqs = pos[:, None] * inv_freq[None, :]
            cos = jnp.cos(freqs)
            sin = jnp.sin(freqs)
            t1 = t[..., ::2]
            t2 = t[..., 1::2]
            rot = jnp.stack([t1 * cos - t2 * sin, t1 * sin + t2 * cos], axis=-1)
            return rot.reshape(t.shape)
        key = jax.random.key(seed)
        ks = jax.random.split(key, 5)
        std = (2.0 / (D_MODEL + D_MODEL)) ** 0.5
        return {'x': jax.random.normal(ks[0], (BATCH, SEQ_LEN, D_MODEL), dtype=jnp.float32), 'Wq': jax.random.normal(ks[1], (D_MODEL, D_MODEL), dtype=jnp.float32) * std, 'Wk': jax.random.normal(ks[2], (D_MODEL, D_MODEL), dtype=jnp.float32) * std, 'Wv': jax.random.normal(ks[3], (D_MODEL, D_MODEL), dtype=jnp.float32) * std, 'Wo': jax.random.normal(ks[4], (D_MODEL, D_MODEL), dtype=jnp.float32) * std}
    _L0_attn_in = _L0_attn_setup()

    def _L0_ffn_setup():
        import jax, jax.numpy as jnp
        import numpy as np
        B, S, D_IN, D_OUT, E, R = (4, 512, 512, 512, 8, 16)
        SCALING = 32.0 / 16.0
        key = jax.random.key(seed)
        ks = jax.random.split(key, 7)
        return {'x': jax.random.normal(ks[0], (B, S, D_IN), jnp.float32), 'base_w': jax.random.normal(ks[1], (D_OUT, D_IN), jnp.float32) * 0.02, 'base_b': jax.random.normal(ks[2], (D_OUT,), jnp.float32) * 0.02, 'router_w': jax.random.normal(ks[3], (E, D_IN), jnp.float32) * 0.02, 'router_b': jax.random.normal(ks[4], (E,), jnp.float32) * 0.02, 'lora_A': jax.random.normal(ks[5], (E, D_IN, R), jnp.float32) * 0.02, 'lora_B': jax.random.normal(ks[6], (E, R, D_OUT), jnp.float32) * 0.02}
    _L0_ffn_in = _L0_ffn_setup()
    _d = {'L0_attn_x': _L0_attn_in['x'], 'L0_attn_Wq': _L0_attn_in['Wq'], 'L0_attn_Wk': _L0_attn_in['Wk'], 'L0_attn_Wv': _L0_attn_in['Wv'], 'L0_attn_Wo': _L0_attn_in['Wo'], 'L0_ffn_base_w': _L0_ffn_in['base_w'], 'L0_ffn_base_b': _L0_ffn_in['base_b'], 'L0_ffn_router_w': _L0_ffn_in['router_w'], 'L0_ffn_router_b': _L0_ffn_in['router_b'], 'L0_ffn_lora_A': _L0_ffn_in['lora_A'], 'L0_ffn_lora_B': _L0_ffn_in['lora_B']}
    _x0 = _d['L0_attn_x']
    _d['L0_attn_x'] = jax.random.normal(jax.random.fold_in(jax.random.key(seed), 1), (2, 2048, 512), dtype=_x0.dtype)
    del _x0
    return _d

def reference(L0_attn_x, L0_attn_Wq, L0_attn_Wk, L0_attn_Wv, L0_attn_Wo, L0_ffn_base_w, L0_ffn_base_b, L0_ffn_router_w, L0_ffn_router_b, L0_ffn_lora_A, L0_ffn_lora_B):

    def _L0_attn_ref(x, Wq, Wk, Wv, Wo):
        import jax, jax.numpy as jnp
        import numpy as np
        import math
        D_MODEL = 512
        NUM_HEADS = 16
        D_K = D_MODEL // NUM_HEADS
        SEQ_LEN = 512
        THETA = 10000.0
        BATCH = 2

        def _rope(t):
            S = t.shape[-2]
            dk = t.shape[-1]
            inv_freq = jnp.exp(-math.log(THETA) * jnp.arange(0, dk, 2, dtype=jnp.float32) / dk)
            pos = jnp.arange(S, dtype=jnp.float32)
            freqs = pos[:, None] * inv_freq[None, :]
            cos = jnp.cos(freqs)
            sin = jnp.sin(freqs)
            t1 = t[..., ::2]
            t2 = t[..., 1::2]
            rot = jnp.stack([t1 * cos - t2 * sin, t1 * sin + t2 * cos], axis=-1)
            return rot.reshape(t.shape)
        B, S, D = x.shape
        H, dk = (NUM_HEADS, D // NUM_HEADS)

        def split_heads(t):
            return t.reshape(B, S, H, dk).transpose(0, 2, 1, 3)
        q = split_heads(x @ Wq.T)
        k = split_heads(x @ Wk.T)
        v = split_heads(x @ Wv.T)
        q = _rope(q)
        k = _rope(k)
        scores = jnp.einsum('bhqd,bhkd->bhqk', q, k) / math.sqrt(dk)
        causal = jnp.tril(jnp.ones((S, S), dtype=bool))
        scores = jnp.where(causal[None, None], scores, -jnp.inf)
        attn = jax.nn.softmax(scores, axis=-1)
        ctx = jnp.einsum('bhqk,bhkd->bhqd', attn, v)
        ctx = ctx.transpose(0, 2, 1, 3).reshape(B, S, D)
        return ctx @ Wo.T

    def _L0_ffn_ref(x, base_w, base_b, router_w, router_b, lora_A, lora_B):
        import jax, jax.numpy as jnp
        import numpy as np
        B, S, D_IN, D_OUT, E, R = (4, 512, 512, 512, 8, 16)
        SCALING = 32.0 / 16.0
        b, s, d_in = x.shape
        n = b * s
        e = lora_A.shape[0]
        d_out = lora_B.shape[-1]
        result = jnp.einsum('bsd,od->bso', x, base_w) + base_b
        logits = jnp.einsum('bsd,ed->bse', x, router_w) + router_b
        probs = jax.nn.softmax(logits.astype(jnp.float32), axis=-1)
        top_vals, top_idx = jax.lax.top_k(probs, 2)
        top_vals = top_vals / jnp.sum(top_vals, axis=-1, keepdims=True)
        top_vals = top_vals.astype(x.dtype)
        flat_idx = top_idx.reshape(n, 2)
        flat_val = top_vals.reshape(n, 2)
        gate = jnp.zeros((n, e), x.dtype).at[jnp.arange(n)[:, None], flat_idx].set(flat_val)
        xf = x.reshape(n, d_in)
        mid = jnp.einsum('nd,edr->ner', xf, lora_A)
        mid = mid * gate[:, :, None]
        lora_out = jnp.einsum('ner,erd->nd', mid, lora_B)
        return result + SCALING * lora_out.reshape(b, s, d_out)
    x = L0_attn_x
    x = x + _L0_attn_ref(_layernorm(x, axis=-1), L0_attn_Wq, L0_attn_Wk, L0_attn_Wv, L0_attn_Wo)
    x = x + _L0_ffn_ref(_layernorm(x, axis=-1), L0_ffn_base_w, L0_ffn_base_b, L0_ffn_router_w, L0_ffn_router_b, L0_ffn_lora_A, L0_ffn_lora_B)
    return x

_drawn_inputs = setup_inputs


def setup_inputs(seed=0):
    import zlib

    import numpy as np

    out = dict(_drawn_inputs(seed))
    spreads = {}
    factors = {'L0_ffn_base_b': 3.172, 'L0_ffn_router_b': 6.112}
    for name, (base, spread) in spreads.items():
        noise = np.random.default_rng([zlib.crc32(name.encode()), seed]).standard_normal(out[name].shape)
        drawn = base * np.exp(spread * noise) if base else spread * noise
        out[name] = jnp.asarray(drawn.astype(out[name].dtype))
    for name, factor in factors.items():
        out[name] = (out[name] * factor).astype(out[name].dtype)
    return out
```

```python
from contextlib import ExitStack

import numpy as np

import concourse.bass as bass
from concourse import mybir

F32 = mybir.dt.float32
F32R = mybir.dt.float32r
ALU = mybir.AluOpType
ACT = mybir.ActivationFunctionType
AX = mybir.AxisListType

P = 128
BATCH, SEQ, DM = 2, 2048, 512
HEADS, DK = 16, 32
EXPERTS, RANK = 8, 16
TOKENS = BATCH * SEQ
KT = DM // P
TT = 512
TILES = TOKENS // TT
SUB = TT // P
HG = 4
GROUPS = BATCH * HEADS // HG
QT = SEQ // TT
KB = SEQ // P
EPS = 1e-5
THETA = 10000.0
LORA_SCALING = 2.0
SCORE_SCALE = 1.0 / float(np.sqrt(DK))
MASKED = -1e38
START = 1

STEPS = [(t, j) for t in range(QT) for j in range((t + 1) * SUB)]
NSTEP = len(STEPS)
UNIT_START = [STEPS.index((t, 0)) for t in range(QT)]
UNIT_END = [STEPS.index((t, (t + 1) * SUB - 1)) for t in range(QT)]
ITEMS = [(t, qi, h, c) for t in range(QT) for qi in range(SUB) for h in range(HG) for c in range(t + 1)]
NITEM = len(ITEMS)
ITEM_END = [max(n for n, it in enumerate(ITEMS) if it[0] == t) for t in range(QT)]
LEAD = 20
PER = NITEM // NSTEP


def items_of_step(s):
    return [((f // NITEM), f % NITEM) for f in range(PER * (s + LEAD), PER * (s + LEAD + 1))]


def wait_alone(eng, semaphore, value, passed):
    eng.wait_ge(semaphore, value)
    eng.sem_inc(passed, 1)


def units_ended_at_step(s):
    return [(n, ITEMS[k][0]) for n, k in items_of_step(s) if k in ITEM_END]


def split_weights(nc, block, sems, jobs, raw, ident=None):
    loaded, hi_done, lo_done = sems

    @block.sync
    def _(sp):
        for n, (src, hi, lo) in enumerate(jobs):
            if n >= 2:
                sp.wait_ge(lo_done, n - 1)
            sp.dma_start(raw[:, n % 2, 0:src.shape[-1]], src).then_inc(loaded[n % 2], 16)

    @block.scalar
    def _(act):
        for n, (src, hi, lo) in enumerate(jobs):
            act.wait_ge(loaded[n % 2], 16 * (n // 2 + 1))
            act.activation(hi, raw[:, n % 2, 0:src.shape[-1]], ACT.Copy).then_inc(hi_done, 1)

    @block.vector
    def _(dve):
        for n, (src, hi, lo) in enumerate(jobs):
            dve.wait_ge(hi_done, n + 1)
            dve.tensor_tensor(lo, raw[:, n % 2, 0:src.shape[-1]], hi.bitcast(F32),
                              ALU.subtract).then_inc(lo_done, 1)


def project(nc, x, wq_t, wk_t, wv_t, rope, qk_scr, v_scr):
    x_v = x.rearrange("(t s p) d -> t p s d", p=P, s=SUB)
    rope_v = rope.rearrange("p c (t n) -> t p c n", n=TT)
    with ExitStack() as ctx:
        def sb(name, shape, dt=F32):
            return ctx.enter_context(nc.sbuf_tensor(name, shape, dt))

        def sem(name):
            return ctx.enter_context(nc.semaphore(name))

        w_raw = sb("p_w_raw", [P, 2, DM])
        w_hi = sb("p_w_hi", [P, KT, 3 * DM], F32R)
        w_lo = sb("p_w_lo", [P, KT, 3 * DM], F32R)
        ident = sb("p_ident", [P, P])
        xb = sb("p_x", [P, 2, SUB, DM])
        stats = sb("p_stats", [P, SUB, 6])
        mv = sb("p_mv", [P, SUB, 2])
        std = sb("p_std", [P, SUB])
        rstd = sb("p_rstd", [P, SUB])
        xt_hi = sb("p_xt_hi", [P, 2, KT, TT], F32R)
        xt_lo = sb("p_xt_lo", [P, 2, KT, TT], F32R)
        tab = sb("p_tab", [P, 2, 3, TT])
        mul = sb("p_mul", [P, 2, 2, 2, TT])
        rot = sb("p_rot", [P, 2, 2, TT])
        rot_hi = sb("p_rot_hi", [P, 2, 2, TT], F32R)
        rot_lo = sb("p_rot_lo", [P, 2, 2, TT], F32R)
        v_st = sb("p_v_st", [P, 2, SUB, DM])
        pair_ps = [ctx.enter_context(nc.psum_tensor(f"p_pair{n}", [P, 2, TT], F32)) for n in range(2)]
        tr_ps = [ctx.enter_context(nc.psum_tensor(f"p_tr{n}", [P, TT], F32)) for n in range(2)]
        v_ps = [ctx.enter_context(nc.psum_tensor(f"p_v{n}", [P, DM], F32)) for n in range(2)]

        w_sems = ([sem("p_w_loaded0"), sem("p_w_loaded1")], sem("p_w_hi_done"), sem("p_w_lo_done"))
        zeroed, ident_done = sem("p_zeroed"), sem("p_ident_done")
        x_loaded = [sem("p_x_loaded0"), sem("p_x_loaded1")]
        tab_loaded = [sem("p_tab_loaded0"), sem("p_tab_loaded1")]
        stats_done, var_done, std_done = sem("p_stats_done"), sem("p_var_done"), sem("p_std_done")
        passed = sem("p_passed")
        rstd_done, xn_done = sem("p_rstd_done"), sem("p_xn_done")
        tr_done, xt_hi_done, xt_lo_done = sem("p_tr_done"), sem("p_xt_hi_done"), sem("p_xt_lo_done")
        pair_done, v_done, v_copied = sem("p_pair_done"), sem("p_v_done"), sem("p_v_copied")
        mul_done, rot_done = sem("p_mul_done"), sem("p_rot_done")
        rot_hi_done, rot_lo_done = sem("p_rot_hi_done"), sem("p_rot_lo_done")
        rot_stored = [sem("p_rot_stored0"), sem("p_rot_stored1")]
        v_stored = [sem("p_v_stored0"), sem("p_v_stored1")]
        AHEAD = 2

        block = ctx.enter_context(nc.Block())
        jobs = [(w[kt * P:(kt + 1) * P, :], w_hi[:, kt, n * DM:(n + 1) * DM], w_lo[:, kt, n * DM:(n + 1) * DM])
                for n, w in enumerate((wq_t, wk_t, wv_t)) for kt in range(KT)]

        @block.sync
        def _(sp):
            for u in range(2):
                sp.dma_start(xb[:, u], x_v[u]).then_inc(x_loaded[u], 16)
                sp.dma_start(tab[:, u], rope_v[u]).then_inc(tab_loaded[u], 16)

        split_weights(nc, block, w_sems, jobs, w_raw)

        @block.gpsimd
        def _(pool):
            for semaphore in (v_done, *rot_stored, *v_stored):
                pool.sem_inc(semaphore, START)
            pool.memset(ident[:, :], 0.0).then_inc(zeroed, 1)
            pool.wait_ge(zeroed, 1)
            pool.affine_select(ident[:, :], ident[:, :], pattern=[[-1, P]], compare_op=ALU.not_equal,
                               fill=1.0, base=0, channel_multiplier=1).then_inc(ident_done, 1)

            def rope_sum(m, par):
                pool.wait_ge(mul_done, m + 1 + AHEAD)
                pool.wait_ge(rot_lo_done, m + 1)
                pool.tensor_tensor(rot[:, par], mul[:, par, :, 0, :], mul[:, par, :, 1, :],
                                   ALU.add).then_inc(rot_done, 1)

            pool.sem_inc(rot_done, AHEAD)
            with pool.Fori(0, TILES) as T:
                for p in range(4):
                    rope_sum(4 * T + p, p % 2)

        @block.sync
        def _(sp):
            with sp.Fori(0, BATCH) as b:
                with sp.Fori(0, 2) as half:
                    for u in range(2):
                        T = 4 * b + 2 * half + u
                        tok = bass.ds(1024 * half + 512 * u, TT)
                        for p in range(4):
                            m = 4 * T + p
                            rows = bass.ds(512 * b + 256 * (p % 2), 256)
                            sp.wait_ge(rot_lo_done, m + 1 + AHEAD)
                            for n, src in enumerate((rot_hi, rot_lo)):
                                dst = qk_scr[2 * (p // 2) + n].rearrange("g r n -> (g r) n")[rows, tok]
                                sp.dma_start(dst.rearrange("(p a) n -> p a n", a=2),
                                             src[:, p % 2].bitcast(F32)).then_inc(rot_stored[p % 2], 16)
                        sp.wait_ge(v_copied, 4 * T + 4 + AHEAD)
                        for hg in range(4):
                            dst = v_scr[4 * b + hg][tok, :].rearrange("(s p) c -> p s c", p=P)
                            sp.dma_start(dst, v_st[:, u, :, hg * P:(hg + 1) * P]).then_inc(v_stored[u], 16)
            for u in range(2):
                sp.wait_ge(rot_stored[u], 32 * 2 * TILES + START)
                sp.wait_ge(v_stored[u], 64 * TILES // 2 + START)

        @block.tensor
        def _(pe):
            pe.wait_ge(ident_done, 1)

            def transposes(T, u):
                pe.wait_ge(xn_done, T + 1)
                for kt in range(KT):
                    if isinstance(T, int) and 4 * T + kt - 1 <= 0:
                        pass
                    else:
                        pe.wait_ge(xt_lo_done, 4 * T + kt - 1)
                    for s in range(SUB):
                        mm = pe.transpose(tr_ps[kt % 2][:, s * P:(s + 1) * P],
                                          xb[:, u, s, kt * P:(kt + 1) * P], ident[:, :])
                    mm.then_inc(tr_done, 1)

            def qk_pair(T, u, p):
                pe.wait_ge(mul_done, 4 * T + p + 1)
                for half in range(2):
                    cols = slice((2 * p + half) * P, (2 * p + half + 1) * P)
                    passes = [(w, a, kt) for w, a in ((w_hi, xt_hi), (w_lo, xt_hi), (w_hi, xt_lo)) for kt in range(KT)]
                    for n, (w, a, kt) in enumerate(passes):
                        mm = pe.matmul(pair_ps[p % 2][:, half, :], w[:, kt, cols], a[:, u, kt, :],
                                       start=(n == 0), stop=(n == len(passes) - 1))
                mm.then_inc(pair_done, 1)

            def v_sub(T, u, s):
                pe.wait_ge(v_copied, 4 * T + s + 1)
                passes = [(a, w, kt) for a, w in ((xt_hi, w_hi), (xt_hi, w_lo), (xt_lo, w_hi)) for kt in range(KT)]
                for n, (a, w, kt) in enumerate(passes):
                    mm = pe.matmul(v_ps[s % 2][:, :], a[:, u, kt, s * P:(s + 1) * P], w[:, kt, 2 * DM:3 * DM],
                                   start=(n == 0), stop=(n == len(passes) - 1))
                mm.then_inc(v_done, 1)

            def tile(T, u, more):
                pe.wait_ge(xt_lo_done, 4 * T + 4)
                for p in range(4):
                    qk_pair(T, u, p)
                    v_sub(T, u, p)
                    if p == 1 and more:
                        transposes(T + 1, 1 - u)

            transposes(0, 0)
            pe.wait_ge(w_sems[2], len(jobs))
            with pe.Fori(0, TILES // 2 - 1) as i:
                for u in range(2):
                    tile(2 * i + u, u, True)
            tile(TILES - 2, 0, True)
            tile(TILES - 1, 1, False)

        @block.scalar
        def _(act):
            def load_x(T, u):
                act.dma_start(xb[:, u], x_v[T]).then_inc(x_loaded[u], 16)

            def load_tab(T, u):
                act.dma_start(tab[:, u], rope_v[T]).then_inc(tab_loaded[u], 16)

            def root(T):
                act.wait_ge(var_done, T + 1)
                act.activation(std[:, :], mv[:, :, 1], ACT.Sqrt, bias=EPS).then_inc(std_done, 1)

            def xt_copy(T, u, kt):
                act.wait_ge(tr_done, 4 * T + kt + 1)
                act.activation(xt_hi[:, u, kt, :], tr_ps[kt % 2][:, :], ACT.Copy).then_inc(xt_hi_done, 1)

            def rot_copy(T, i, p):
                act.wait_ge(rot_done, 4 * T + p + 1 + AHEAD)
                act.wait_ge(rot_stored[p % 2], 32 * (2 * T + p // 2) + START)
                act.activation(rot_hi[:, p % 2], rot[:, p % 2], ACT.Copy).then_inc(rot_hi_done, 1)

            def v_copy(T, i, u, s):
                act.wait_ge(v_done, 4 * T + s + 1 + START)
                if s == 0:
                    act.wait_ge(v_stored[u], 64 * i + START)
                act.activation(v_st[:, u, s, :], v_ps[s % 2][:, :], ACT.Copy).then_inc(v_copied, 1)

            def tile(T, i, u, more, load):
                if load:
                    load_x(T + 2, u)
                if more:
                    root(T + 1)
                v_copy(T, i, u, 0)
                rot_copy(T, i, 0)
                v_copy(T, i, u, 1)
                if more:
                    act.wait_ge(v_done, 4 * T + START)
                    for kt in range(KT):
                        xt_copy(T + 1, 1 - u, kt)
                rot_copy(T, i, 1)
                v_copy(T, i, u, 2)
                rot_copy(T, i, 2)
                v_copy(T, i, u, 3)
                rot_copy(T, i, 3)
                if load:
                    act.wait_ge(mul_done, 4 * T + 4 + AHEAD)
                    load_tab(T + 2, u)

            root(0)
            for kt in range(KT):
                xt_copy(0, 0, kt)
            act.sem_inc(v_copied, AHEAD)
            with act.Fori(0, TILES // 2 - 1) as i:
                for u in range(2):
                    tile(2 * i + u, i, u, True, True)
            tile(TILES - 2, TILES // 2 - 1, 0, True, False)
            tile(TILES - 1, TILES // 2 - 1, 1, False, False)

        @block.vector
        def _(dve):
            def layer_norm(T, i, u):
                dve.wait_ge(x_loaded[u], 16 * i + 16)
                if not (isinstance(T, int) and T == 0):
                    dve.wait_ge(xn_done, T)
                for s in range(SUB):
                    ins = dve.bn_stats(stats[:, s, :], xb[:, u, s, :])
                ins.then_inc(stats_done, 1)
                wait_alone(dve, stats_done, T + 1, passed)
                for s in range(SUB):
                    ins = dve.bn_aggr(mv[:, s, :], stats[:, s, :])
                ins.then_inc(var_done, 1)
                dve.wait_ge(std_done, T + 1)
                dve.reciprocal(rstd[:, :], std[:, :]).then_inc(rstd_done, 1)
                dve.wait_ge(rstd_done, T + 1)
                for s in range(SUB):
                    ins = dve.tensor_scalar(xb[:, u, s, :], xb[:, u, s, :], mv[:, s, 0:1], rstd[:, s:s + 1],
                                            ALU.subtract, ALU.mult)
                ins.then_inc(xn_done, 1)

            def xt_rest(T, u, kt):
                dve.wait_ge(xt_hi_done, 4 * T + kt + 1)
                dve.tensor_tensor(xt_lo[:, u, kt, :], tr_ps[kt % 2][:, :], xt_hi[:, u, kt, :].bitcast(F32),
                                  ALU.subtract).then_inc(xt_lo_done, 1)

            def rope_mul(T, i, u, p):
                if p == 0:
                    dve.wait_ge(tab_loaded[u], 16 * i + 16)
                dve.wait_ge(pair_done, 4 * T + p + 1)
                dve.wait_ge(rot_done, 4 * T + p + 1)
                even, odd = (pair_ps[p % 2][:, n:n + 1, :].to_broadcast([P, 2, TT]) for n in range(2))
                dve.tensor_tensor(mul[:, p % 2, :, 0, :], even, tab[:, u, 1:3, :], ALU.mult)
                dve.tensor_tensor(mul[:, p % 2, :, 1, :], odd, tab[:, u, 0:2, :], ALU.mult).then_inc(mul_done, 1)

            def rot_rest(T, p):
                dve.wait_ge(rot_hi_done, 4 * T + p + 1)
                dve.tensor_tensor(rot_lo[:, p % 2], rot[:, p % 2], rot_hi[:, p % 2].bitcast(F32),
                                  ALU.subtract).then_inc(rot_lo_done, 1)

            def tile(T, i, u, more):
                if more:
                    layer_norm(T + 1, i + u, 1 - u)
                rope_mul(T, i, u, 0)
                rope_mul(T, i, u, 1)
                rot_rest(T, 0)
                if more:
                    for kt in range(KT):
                        xt_rest(T + 1, 1 - u, kt)
                rope_mul(T, i, u, 2)
                rot_rest(T, 1)
                rope_mul(T, i, u, 3)
                rot_rest(T, 2)
                rot_rest(T, 3)

            dve.sem_inc(mul_done, AHEAD)
            dve.sem_inc(rot_lo_done, AHEAD)
            layer_norm(0, 0, 0)
            for kt in range(KT):
                xt_rest(0, 0, kt)
            with dve.Fori(0, TILES // 2 - 1) as i:
                for u in range(2):
                    tile(2 * i + u, i, u, True)
            tile(TILES - 2, TILES // 2 - 1, 0, True)
            tile(TILES - 1, TILES // 2 - 1, 1, False)


def attend(nc, qk_scr, v_scr, ctx_scr):
    with ExitStack() as ctx:
        def sb(name, shape, dt=F32):
            return ctx.enter_context(nc.sbuf_tensor(name, shape, dt))

        def sem(name):
            return ctx.enter_context(nc.semaphore(name))

        q_stack = [sb(f"a_q_stack{n}", [P, HG, SEQ], F32R) for n in range(2)]
        k_stack = [sb(f"a_k_stack{n}", [P, HG, SEQ], F32R) for n in range(2)]
        vb = sb("a_v", [P, 2, KB, P])
        probs = sb("a_probs", [P, 4, HG, TT])
        ctx_st = sb("a_ctx_st", [P, 2, TT])
        sum_t = sb("a_sum_t", [P, TT])
        rsum = sb("a_rsum", [P, TT // 32])
        rsum_b = sb("a_rsum_b", [P, TT])
        mask = sb("a_mask", [P, TT])
        ones = sb("a_ones", [P, DK])
        ident = sb("a_ident", [P, P])
        part = sb("a_part", [P, HG * SUB, QT])
        neg_max = sb("a_neg_max", [P, HG * SUB])
        neg_parts = sb("a_neg_parts", [P, HG, 2, SUB])
        neg_rows = sb("a_neg_rows", [2 * HG * SUB, 2, P])
        st_ps = ctx.enter_context(nc.psum_tensor("a_st", [P, HG, TT], F32))
        mx_ps = [ctx.enter_context(nc.psum_tensor(f"a_mx{n}", [P, TT], F32)) for n in range(2)]
        av_ps = ctx.enter_context(nc.psum_tensor("a_av", [P, TT], F32))
        sum_ps = ctx.enter_context(nc.psum_tensor("a_sum", [P, TT], F32))

        loaded = [sem("a_loaded0"), sem("a_loaded1")]
        shift_loaded = [sem("a_shift_loaded0"), sem("a_shift_loaded1")]
        consts_done, zeroed = sem("a_consts_done"), sem("a_zeroed")
        st_done, exp_done, masked = sem("a_st_done"), sem("a_exp_done"), sem("a_masked")
        step_done, out_done = sem("a_step_done"), sem("a_out_done")
        item_done, max_done = sem("a_item_done"), sem("a_max_done")
        dve_passed, pool_passed = sem("a_dve_passed"), sem("a_pool_passed")
        reduced, rounded = sem("a_reduced"), sem("a_rounded")
        sum_turned, rsum_done, rsum_turned = sem("a_sum_turned"), sem("a_rsum_done"), sem("a_rsum_turned")
        neg_done, neg_turned, rows_done = sem("a_neg_done"), sem("a_neg_turned"), sem("a_rows_done")
        ctx_stored = [sem("a_ctx_stored0"), sem("a_ctx_stored1")]
        LOADS, SHIFTS = 16 * 8, 16 * HG
        RING = 4
        AHEAD = 2
        BANKS = HG

        block = ctx.enter_context(nc.Block())

        @block.sync
        def _(sp):
            def load_group(g, par):
                for n, kind in enumerate((0, 0, 1)):
                    sp.dma_start(q_stack[par][32 * n:32 * n + 32].bitcast(F32),
                                 qk_scr[kind, g].rearrange("(h r) n -> r h n", r=DK)).then_inc(loaded[par], 16)
                for n, kind in enumerate((2, 3, 2)):
                    sp.dma_start(k_stack[par][32 * n:32 * n + 32].bitcast(F32),
                                 qk_scr[kind, g].rearrange("(h r) n -> r h n", r=DK)).then_inc(loaded[par], 16)
                v_rows = v_scr[g].rearrange("(a j p) c -> a p j c", p=P, a=2)
                for n in range(2):
                    sp.dma_start(vb[:, par, n * KB // 2:(n + 1) * KB // 2], v_rows[n]).then_inc(loaded[par], 16)

            def shift_rows(g, par, t):
                sp.wait_ge(rows_done, 4 * g + t + 1)
                for h in range(HG):
                    dst = q_stack[par][96:98, h, t * TT:(t + 1) * TT].bitcast(F32)
                    sp.dma_start(dst.rearrange("p (q c) -> p q c", c=P),
                                 neg_rows[8 * h:8 * h + 8, t % 2, :]).then_inc(shift_loaded[t % 2], 16)

            def group(g, par, last):
                if not last:
                    sp.wait_ge(step_done, NSTEP * g + RING)
                    load_group(g + 1, 1 - par)
                for s in range(NSTEP):
                    for nxt, t in units_ended_at_step(s):
                        if not (nxt and last):
                            shift_rows(g + nxt, (par + nxt) % 2, t)
                    if s in UNIT_END:
                        t = STEPS[s][0]
                        sp.wait_ge(out_done, 4 * g + t + 1 + START)
                        sp.dma_start(ctx_scr[g][:, t * TT:(t + 1) * TT], ctx_st[:, t % 2]).then_inc(ctx_stored[t % 2], 16)

            load_group(0, 0)
            for t in range(QT):
                if ITEM_END[t] < PER * LEAD:
                    shift_rows(0, 0, t)
            with sp.Fori(0, GROUPS // 2 - 1) as i:
                for par in range(2):
                    group(2 * i + par, par, False)
            group(GROUPS - 2, 0, False)
            group(GROUPS - 1, 1, True)
            for n in range(2):
                sp.wait_ge(ctx_stored[n], 16 * GROUPS * QT // 2 + START)

        @block.gpsimd
        def _(pool):
            for semaphore in (out_done, neg_turned, *shift_loaded, *ctx_stored):
                pool.sem_inc(semaphore, START)
            pool.memset(ident[:, :], 0.0).then_inc(zeroed, 1)
            pool.wait_ge(zeroed, 1)
            pool.memset(mask[:, :], 0.0).then_inc(zeroed, 1)
            pool.wait_ge(zeroed, 2)
            pool.affine_select(ident[:, :], ident[:, :], pattern=[[-1, P]], compare_op=ALU.not_equal,
                               fill=1.0, base=0, channel_multiplier=1).then_inc(consts_done, 1)
            pool.affine_select(mask[:, TT - P:TT], mask[:, TT - P:TT], pattern=[[-1, P]], compare_op=ALU.is_ge,
                               fill=MASKED, base=0, channel_multiplier=1).then_inc(consts_done, 1)

            with pool.Fori(0, GROUPS) as g:
                for s, (t, j) in enumerate(STEPS):
                    if j < t * SUB:
                        continue
                    q0 = (j - t * SUB) * P
                    for h in range(HG):
                        wait_alone(pool, exp_done, HG * NSTEP * g + HG * s + h + 1 + BANKS, pool_passed)
                        tri = probs[:, s % 4, h, q0:q0 + P]
                        pool.affine_select(tri, tri, pattern=[[1, P]], compare_op=ALU.is_ge, fill=0.0,
                                           base=0, channel_multiplier=-1).then_inc(masked, 1)

        @block.tensor
        def _(pe):
            def item(g, par, use, k):
                t, qi, h, c = ITEMS[k]
                width = TT if c < t else (qi + 1) * P
                if k == 0:
                    pe.wait_ge(loaded[par], LOADS * use + LOADS)
                pe.wait_ge(max_done, NITEM * g + k + 1)
                pe.matmul(mx_ps[k % 2][:, 0:width], q_stack[par][0:96, h, t * TT + qi * P:t * TT + (qi + 1) * P],
                          k_stack[par][0:96, h, c * TT:c * TT + width], start=True, stop=True).then_inc(item_done, 1)

            def turn_maxima(g, t, items):
                pe.wait_ge(neg_done, 4 * g + t + 1)
                pe.wait_ge(max_done, items - 1 + AHEAD)
                pe.transpose(mx_ps[0][0:2 * HG * SUB, 0:P], neg_parts[:, :, :, :].rearrange("p h n q -> p (h n q)"), ident[:, :]).then_inc(neg_turned, 1)

            def scores(g, par, i, s, h):
                t, j = STEPS[s]
                q0 = max(0, j - t * SUB) * P
                if j == 0 and h == 0:
                    pe.wait_ge(shift_loaded[t % 2], SHIFTS * (2 * g + t // 2 + 1) + START)
                pe.wait_ge(exp_done, HG * NSTEP * g + HG * s + h + 1)
                pe.matmul(st_ps[:, h, q0:TT], k_stack[par][0:98, h, j * P:(j + 1) * P],
                          q_stack[par][0:98, h, t * TT + q0:(t + 1) * TT], start=True, stop=True).then_inc(st_done, 1)

            def values(g, par, s):
                t, j = STEPS[s]
                q0 = max(0, j - t * SUB) * P
                first, last = j == 0, s in UNIT_END
                if first:
                    pe.wait_ge(out_done, 4 * g + t + START)
                for out, weights in ((av_ps, vb[:, par, j, :]), (sum_ps, None)):
                    for h in range(HG):
                        if weights is not None:
                            if j >= t * SUB:
                                diag = SUB * t + j - t * SUB
                                pe.wait_ge(masked, HG * SUB * QT * g + HG * diag + h + 1)
                            else:
                                pe.wait_ge(exp_done, HG * NSTEP * g + HG * s + h + 1 + BANKS)
                        w = ones[:, :] if weights is None else weights[:, h * DK:(h + 1) * DK]
                        mm = pe.matmul(out[h * DK:(h + 1) * DK, q0:TT], w, probs[:, s % 4, h, q0:TT],
                                       start=first, stop=last, tile_position=(0, h * DK))
                mm.then_inc(step_done, 1)

            def group(g, par, i, last):
                for s in range(NSTEP):
                    items = [(n, k) for n, k in items_of_step(s) if not (n and last)]
                    for n, t in units_ended_at_step(s - 2) if s > 1 else []:
                        if items:
                            pe.wait_ge(rows_done, 4 * (g + n) + t + 1)
                    for h in range(HG):
                        if h < len(items):
                            n, k = items[h]
                            item(g + n, (par + n) % 2, i + (1 if n and par else 0), k)
                        if s + 1 < NSTEP:
                            scores(g, par, i, s + 1, h)
                        elif not last:
                            scores(g + 1, 1 - par, i, 0, h)
                    for n, t in units_ended_at_step(s - 1) if s else []:
                        if not (n and last):
                            turn_maxima(g + n, t, NITEM * g + min(PER * (s + LEAD + 1), NITEM if last else 2 * NITEM))
                    values(g, par, s)

            pe.wait_ge(consts_done, 5)
            pe.wait_ge(loaded[0], LOADS)
            for k in range(PER * LEAD):
                item(0, 0, 0, k)
                for t in range(QT):
                    if k == ITEM_END[t] + PER and k < PER * LEAD:
                        turn_maxima(0, t, k + 1)
                        pe.wait_ge(rows_done, t + 1)
            for h in range(HG):
                scores(0, 0, 0, 0, h)
            with pe.Fori(0, GROUPS // 2 - 1) as i:
                for par in range(2):
                    group(2 * i + par, par, i, False)
            group(GROUPS - 2, 0, GROUPS // 2 - 1, False)
            group(GROUPS - 1, 1, GROUPS // 2 - 1, True)

        @block.scalar
        def _(act):
            act.sem_inc(exp_done, BANKS)
            with act.Fori(0, GROUPS) as g:
                for s, (t, j) in enumerate(STEPS):
                    q0 = max(0, j - t * SUB) * P
                    act.wait_ge(step_done, NSTEP * g + s + 1)
                    for h in range(HG):
                        act.wait_ge(st_done, HG * NSTEP * g + HG * s + h + 1)
                        act.activation(probs[:, s % 4, h, q0:TT], st_ps[:, h, q0:TT], ACT.Exp,
                                       scale=SCORE_SCALE).then_inc(exp_done, 1)

        @block.vector
        def _(dve):
            def item_max(g, k):
                t, qi, h, c = ITEMS[k]
                if c < t:
                    dve.wait_ge(item_done, NITEM * g + k + 1)
                else:
                    wait_alone(dve, item_done, NITEM * g + k + 1, dve_passed)
                out = part[:, h * SUB + qi, c:c + 1]
                if c < t:
                    dve.tensor_reduce(out, mx_ps[k % 2][:, :], AX.X, ALU.max).then_inc(max_done, 1)
                else:
                    width = (qi + 1) * P
                    dve.tensor_tensor_reduce(out=mx_ps[k % 2][:, 0:width], in0=mx_ps[k % 2][:, 0:width],
                                             in1=mask[:, TT - width:TT], scale=1.0, scalar=3.0 * MASKED,
                                             op0=ALU.add, op1=ALU.max, accum_out=out).then_inc(max_done, 1)

            def unit_max(g, t, items):
                dve.wait_ge(max_done, items + AHEAD)
                dve.wait_ge(neg_turned, 4 * g + t + START)
                dve.tensor_reduce(neg_max[:, :], part[:, :, 0:t + 1], AX.X, ALU.max, negate=True).then_inc(reduced, 1)
                dve.wait_ge(reduced, 4 * g + t + 1)
                neg = neg_max[:, :].rearrange("p (h q) -> p h q", q=SUB)
                dve.tensor_copy(neg_parts[:, :, 0, :].bitcast(F32R), neg).then_inc(rounded, 1)
                dve.wait_ge(rounded, 4 * g + t + 1)
                dve.tensor_tensor(neg_parts[:, :, 1, :].bitcast(F32R), neg, neg_parts[:, :, 0, :],
                                  ALU.subtract).then_inc(neg_done, 1)

            def unit_rows(g, t):
                dve.wait_ge(neg_turned, 4 * g + t + 1 + START)
                dve.wait_ge(shift_loaded[t % 2], SHIFTS * (2 * g + t // 2) + START)
                dve.tensor_copy(neg_rows[:, t % 2, :].bitcast(F32R), mx_ps[0][0:32, 0:P]).then_inc(rows_done, 1)

            def unit_out(g, s):
                t = STEPS[s][0]
                U = 4 * g + t
                dve.wait_ge(step_done, NSTEP * g + s + 1 + RING)
                dve.transpose(sum_t[:, :], sum_ps[:, :]).then_inc(sum_turned, 1)
                dve.wait_ge(sum_turned, U + 1)
                dve.reciprocal(rsum[:, :], sum_t[:, :].rearrange("p (b i) -> p b i", i=32)[:, :, 0]).then_inc(rsum_done, 1)
                dve.wait_ge(rsum_done, U + 1)
                dve.transpose(rsum_b[:, :], rsum[:, :].unsqueeze(2).to_broadcast([P, TT // 32, 32])).then_inc(rsum_turned, 1)
                dve.wait_ge(rsum_turned, U + 1)
                dve.wait_ge(ctx_stored[t % 2], 16 * (2 * g + t // 2) + START)
                dve.tensor_tensor(ctx_st[:, t % 2], av_ps[:, :], rsum_b[:, :], ALU.mult).then_inc(out_done, 1)

            def group(g, last):
                for s in range(NSTEP):
                    for n, k in items_of_step(s):
                        if not (n and last):
                            item_max(g + n, k)
                    for n, t in units_ended_at_step(s):
                        if not (n and last):
                            unit_max(g + n, t, NITEM * g + PER * (s + LEAD + 1))
                    for n, t in units_ended_at_step(s - 1) if s else []:
                        if not (n and last):
                            unit_rows(g + n, t)
                    if s in UNIT_END:
                        unit_out(g, s)

            dve.memset(ones[:, :], 1.0).then_inc(consts_done, 1)
            for n in range(2):
                dve.memset(k_stack[n][96:98].bitcast(F32), 1.0).then_inc(consts_done, 1)
            dve.sem_inc(max_done, AHEAD)
            dve.sem_inc(step_done, RING)
            dve.wait_ge(consts_done, 5)
            for k in range(PER * LEAD):
                item_max(0, k)
                for t in range(QT):
                    if k == ITEM_END[t]:
                        unit_max(0, t, k + 1)
                    if k == ITEM_END[t] + PER:
                        unit_rows(0, t)
            with dve.Fori(0, GROUPS - 1) as g:
                group(g, False)
            group(GROUPS - 1, True)


def finish(nc, x, ctx_scr, wo_t, base_t, base_b, router_t, router_b, lora_a, lora_b, out):
    x_v = x.rearrange("(t s p) d -> t p s d", p=P, s=SUB)
    out_v = out.rearrange("(t s p) d -> t p s d", p=P, s=SUB)
    ctx_v = ctx_scr.rearrange("(b k) p n -> b p k n", k=KT)
    E = EXPERTS
    with ExitStack() as ctx:
        def sb(name, shape, dt=F32):
            return ctx.enter_context(nc.sbuf_tensor(name, shape, dt))

        def sem(name):
            return ctx.enter_context(nc.semaphore(name))

        def psum(name, shape):
            return ctx.enter_context(nc.psum_tensor(name, shape, F32))

        w_raw = sb("f_w_raw", [P, 2, DM])
        wo_hi, wo_lo = sb("f_wo_hi", [P, KT, DM], F32R), sb("f_wo_lo", [P, KT, DM], F32R)
        base_hi, base_lo = sb("f_base_hi", [P, KT, DM], F32R), sb("f_base_lo", [P, KT, DM], F32R)
        a_hi, a_lo = sb("f_a_hi", [P, KT, P], F32R), sb("f_a_lo", [P, KT, P], F32R)
        r_hi, r_lo = sb("f_r_hi", [P, KT, E], F32R), sb("f_r_lo", [P, KT, E], F32R)
        b_hi, b_lo = sb("f_b_hi", [P, DM], F32R), sb("f_b_lo", [P, DM], F32R)
        bias = sb("f_bias", [P, DM])
        r_bias = sb("f_r_bias", [P, E])
        ident = sb("f_ident", [P, P])
        lower = sb("f_lower", [P, E, E])
        cin = sb("f_ctx", [P, KT, TT])
        c_hi, c_lo = sb("f_c_hi", [P, 2, KT, TT], F32R), sb("f_c_lo", [P, 2, KT, TT], F32R)
        xin = sb("f_x", [P, 2, SUB, DM])
        xn = sb("f_xn", [P, SUB, DM])
        xt_hi, xt_lo = sb("f_xt_hi", [P, 2, KT, TT], F32R), sb("f_xt_lo", [P, 2, KT, TT], F32R)
        stats, mv = sb("f_stats", [P, SUB, 6]), sb("f_mv", [P, SUB, 2])
        std, rstd = sb("f_std", [P, SUB]), sb("f_rstd", [P, SUB])
        logit, shifted, ex, prob = (sb(f"f_g{n}", [P, SUB, E]) for n in range(4))
        rank, picked, gate = (sb(f"f_h{n}", [P, SUB, E]) for n in range(3))
        top, den, rden, psum2, rpsum2 = (sb(f"f_s{n}", [P, SUB]) for n in range(5))
        above, ties = sb("f_above", [P, SUB, E, E]), sb("f_ties", [P, SUB, E, E])
        mid = sb("f_mid", [P, SUB, P])
        mt_hi, mt_lo = sb("f_mt_hi", [P, TT], F32R), sb("f_mt_lo", [P, TT], F32R)
        y = sb("f_y", [P, 2, SUB, DM])
        wo_ps = [psum(f"f_wo_ps{n}", [P, DM]) for n in range(2)]
        tr_ps = [psum(f"f_tr_ps{n}", [P, TT]) for n in range(2)]
        out_ps = [psum(f"f_out_ps{n}", [P, DM]) for n in range(2)]
        mid_ps = psum("f_mid_ps", [P, TT])
        lg_ps = psum("f_lg_ps", [P, DM])

        w_sems = ([sem("f_w_loaded0"), sem("f_w_loaded1")], sem("f_w_hi_done"), sem("f_w_lo_done"))
        zeroed, consts_done, bias_loaded = sem("f_zeroed"), sem("f_consts_done"), sem("f_bias_loaded")
        ctx_loaded = sem("f_ctx_loaded")
        x_loaded = [sem("f_x_loaded0"), sem("f_x_loaded1")]
        c_hi_done, c_lo_done = sem("f_c_hi_done"), sem("f_c_lo_done")
        wo_done, added, stats_done, var_done = sem("f_wo_done"), sem("f_added"), sem("f_stats_done"), sem("f_var_done")
        std_done, rstd_done, xn_done, biased = sem("f_std_done"), sem("f_rstd_done"), sem("f_xn_done"), sem("f_biased")
        tr_done, xt_hi_done, xt_lo_done = sem("f_tr_done"), sem("f_xt_hi_done"), sem("f_xt_lo_done")
        router_done, mid_done, gated = sem("f_router_done"), sem("f_mid_done"), sem("f_gated")
        passed = sem("f_passed")
        link, shift_done, ex_done = sem("f_link"), sem("f_shift_done"), sem("f_ex_done")
        mt_done, mt_hi_done, mt_lo_done = sem("f_mt_done"), sem("f_mt_hi_done"), sem("f_mt_lo_done")
        out_done, y_done = sem("f_out_done"), sem("f_y_done")
        y_stored = [sem("f_y_stored0"), sem("f_y_stored1")]
        AHEAD = 2
        FREE = SUB + START

        block = ctx.enter_context(nc.Block())

        @block.sync
        def _(sp):
            sp.dma_start(bias[:, :], base_b.to_broadcast([P, DM])).then_inc(bias_loaded, 16)
            sp.dma_start(r_bias[:, :], router_b.to_broadcast([P, E])).then_inc(bias_loaded, 16)

        rows = [slice(kt * P, (kt + 1) * P) for kt in range(KT)]
        jobs = [(wo_t[rows[kt], :], wo_hi[:, kt, :], wo_lo[:, kt, :]) for kt in range(KT)]
        jobs += [(base_t[rows[kt], :], base_hi[:, kt, :], base_lo[:, kt, :]) for kt in range(KT)]
        jobs += [(lora_a[rows[kt], :], a_hi[:, kt, :], a_lo[:, kt, :]) for kt in range(KT)]
        jobs += [(router_t[rows[kt], :], r_hi[:, kt, :], r_lo[:, kt, :]) for kt in range(KT)]
        jobs += [(lora_b, b_hi[:, :], b_lo[:, :])]
        split_weights(nc, block, w_sems, jobs, w_raw)

        @block.sync
        def _(sp):
            with sp.Fori(0, BATCH) as b:
                with sp.Fori(0, QT // 2) as half:
                    for u in range(2):
                        T = 4 * b + 2 * half + u
                        i = 2 * b + half
                        sp.wait_ge(c_lo_done, T + START)
                        sp.dma_start(cin[:, :, :], ctx_v[b, :, :, bass.ds(1024 * half + 512 * u, TT)]).then_inc(ctx_loaded, 16)
                        sp.wait_ge(y_done, 4 * T + START)
                        sp.dma_start(xin[:, u], x_v[T]).then_inc(x_loaded[u], 16)

        @block.gpsimd
        def _(pool):
            for semaphore in (c_lo_done, gated, mt_lo_done, out_done, *y_stored):
                pool.sem_inc(semaphore, START)
            pool.memset(ident[:, :], 0.0).then_inc(zeroed, 1)
            pool.wait_ge(zeroed, 1)
            pool.memset(lower[:, :, :], 1.0).then_inc(zeroed, 1)
            pool.wait_ge(zeroed, 2)
            pool.affine_select(ident[:, :], ident[:, :], pattern=[[-1, P]], compare_op=ALU.not_equal,
                               fill=1.0, base=0, channel_multiplier=1).then_inc(consts_done, 1)
            pool.affine_select(lower[:, :, :], lower[:, :, :], pattern=[[1, E], [-1, E]], compare_op=ALU.is_gt,
                               fill=0.0, base=0, channel_multiplier=0).then_inc(consts_done, 1)
            pool.wait_ge(bias_loaded, 32)
            with pool.Fori(0, TILES // 2) as i:
                for u in range(2):
                    T = 2 * i + u
                    pool.wait_ge(xn_done, T + 1)
                    for s in range(SUB):
                        ins = pool.tensor_tensor(xin[:, u, s, :], xin[:, u, s, :], bias[:, :], ALU.add)
                    ins.then_inc(biased, 1)

        @block.tensor
        def _(pe):
            def product(out, pairs, done):
                for n, (w, a) in enumerate(pairs):
                    mm = pe.matmul(out, w, a, start=(n == 0), stop=(n == len(pairs) - 1))
                if done is not None:
                    mm.then_inc(done, 1)

            def attention_out(T, u, s):
                m = 4 * T + s
                if s == 0:
                    pe.wait_ge(c_lo_done, T + 1 + START)
                pe.wait_ge(added, m + 1)
                tok = slice(s * P, (s + 1) * P)
                product(wo_ps[s % 2][:, :], [(c[:, u, kt, tok], w[:, kt, :]) for c, w in
                        ((c_hi, wo_hi), (c_hi, wo_lo), (c_lo, wo_hi)) for kt in range(KT)], wo_done)

            def transposes(T, kt):
                if kt == 0:
                    pe.wait_ge(xn_done, T + 1)
                if not (isinstance(T, int) and 4 * T + kt - 1 <= 0):
                    pe.wait_ge(xt_lo_done, 4 * T + kt - 1)
                for s in range(SUB):
                    mm = pe.transpose(tr_ps[kt % 2][:, s * P:(s + 1) * P], xn[:, s, kt * P:(kt + 1) * P], ident[:, :])
                mm.then_inc(tr_done, 1)

            def router_and_mid(T, u):
                pe.wait_ge(xt_lo_done, 4 * T + 4)
                pe.wait_ge(gated, T + START)
                for s in range(SUB):
                    tok = slice(s * P, (s + 1) * P)
                    product(lg_ps[:, s * E:(s + 1) * E], [(a[:, u, kt, tok], w[:, kt, :]) for a, w in
                            ((xt_hi, r_hi), (xt_hi, r_lo), (xt_lo, r_hi)) for kt in range(KT)],
                            router_done if s == SUB - 1 else None)
                pe.wait_ge(mt_lo_done, T + START)
                for s in range(SUB):
                    tok = slice(s * P, (s + 1) * P)
                    product(mid_ps[:, tok], [(a[:, u, kt, tok], w[:, kt, :]) for a, w in
                            ((xt_hi, a_hi), (xt_hi, a_lo), (xt_lo, a_hi)) for kt in range(KT)],
                            mid_done if s == SUB - 1 else None)

            def base(T, u, s):
                pe.wait_ge(y_done, 4 * T + s - 1 + FREE)
                pairs = [(a[:, u, kt, s * P:(s + 1) * P], w[:, kt, :]) for a, w in
                         ((xt_hi, base_hi), (xt_hi, base_lo), (xt_lo, base_hi)) for kt in range(KT)]
                for n, (w, a) in enumerate(pairs):
                    pe.matmul(out_ps[s % 2][:, :], w, a, start=(n == 0), stop=False)

            def turn_mid(T):
                pe.wait_ge(gated, T + 1 + START)
                for s in range(SUB):
                    mm = pe.transpose(mid_ps[:, s * P:(s + 1) * P], mid[:, s, :], ident[:, :])
                mm.then_inc(mt_done, 1)

            def experts(T, s):
                pe.wait_ge(mt_lo_done, T + 1 + START)
                tok = slice(s * P, (s + 1) * P)
                pairs = ((mt_hi, b_hi), (mt_hi, b_lo), (mt_lo, b_hi))
                for n, (a, w) in enumerate(pairs):
                    mm = pe.matmul(out_ps[s % 2][:, :], a[:, tok], w[:, :], start=False, stop=(n == len(pairs) - 1))
                mm.then_inc(out_done, 1)

            def tile(T, u, more):
                router_and_mid(T, u)
                if more:
                    for s in range(SUB):
                        attention_out(T + 1, 1 - u, s)
                base(T, u, 0)
                base(T, u, 1)
                turn_mid(T)
                experts(T, 0)
                experts(T, 1)
                base(T, u, 2)
                if more:
                    transposes(T + 1, 0)
                    transposes(T + 1, 1)
                experts(T, 2)
                base(T, u, 3)
                if more:
                    transposes(T + 1, 2)
                    transposes(T + 1, 3)
                experts(T, 3)

            pe.wait_ge(consts_done, 2)
            pe.wait_ge(w_sems[2], len(jobs))
            for s in range(SUB):
                attention_out(0, 0, s)
            for kt in range(KT):
                transposes(0, kt)
            with pe.Fori(0, TILES // 2 - 1) as i:
                for u in range(2):
                    tile(2 * i + u, u, True)
            tile(TILES - 2, 0, True)
            tile(TILES - 1, 1, False)

        @block.scalar
        def _(act):
            def ctx_copy(T, u):
                act.wait_ge(ctx_loaded, 16 * T + 16)
                act.activation(c_hi[:, u], cin[:, :, :], ACT.Copy).then_inc(c_hi_done, 1)

            def root(T):
                act.wait_ge(var_done, T + 1)
                act.activation(std[:, :], mv[:, :, 1], ACT.Sqrt, bias=EPS).then_inc(std_done, 1)

            def xt_copy(T, u, kt):
                act.wait_ge(tr_done, 4 * T + kt + 1)
                act.activation(xt_hi[:, u, kt, :], tr_ps[kt % 2][:, :], ACT.Copy).then_inc(xt_hi_done, 1)

            def tile(T, u, more, load):
                act.wait_ge(shift_done, T + 1)
                act.activation(ex[:, :, :], shifted[:, :, :], ACT.Exp).then_inc(ex_done, 1)
                if load:
                    act.wait_ge(wo_done, 4 * T + 4)
                    ctx_copy(T + 2, u)
                if more:
                    root(T + 1)
                act.wait_ge(mt_done, T + 1)
                act.wait_ge(out_done, 4 * T + START)
                act.activation(mt_hi[:, :], mid_ps[:, :], ACT.Copy).then_inc(mt_hi_done, 1)
                if more:
                    for kt in range(KT):
                        xt_copy(T + 1, 1 - u, kt)
                act.wait_ge(y_done, 4 * T + 4 + FREE)
                act.dma_start(out_v[T], y[:, u]).then_inc(y_stored[u], 16)

            ctx_copy(0, 0)
            ctx_copy(1, 1)
            root(0)
            for kt in range(KT):
                xt_copy(0, 0, kt)
            with act.Fori(0, TILES // 2 - 1) as i:
                for u in range(2):
                    tile(2 * i + u, u, True, True)
            tile(TILES - 2, 0, True, False)
            tile(TILES - 1, 1, False, False)
            for u in range(2):
                act.wait_ge(y_stored[u], 16 * TILES // 2 + START)

        @block.vector
        def _(dve):
            LINKS = 14

            def ctx_rest(T, u):
                dve.wait_ge(c_hi_done, T + 1)
                dve.tensor_tensor(c_lo[:, u], cin[:, :, :], c_hi[:, u].bitcast(F32), ALU.subtract).then_inc(c_lo_done, 1)

            def add_and_norm(T, i, u):
                dve.wait_ge(x_loaded[u], 16 * i + 16)
                for s in range(SUB):
                    dve.wait_ge(wo_done, 4 * T + s + 1)
                    xs = xin[:, u, s, :]
                    dve.tensor_tensor(xs, wo_ps[s % 2][:, :], xs, ALU.add).then_inc(added, 1)
                    dve.wait_ge(added, 4 * T + s + 1 + AHEAD)
                    ins = dve.bn_stats(stats[:, s, :], xs)
                ins.then_inc(stats_done, 1)
                wait_alone(dve, stats_done, T + 1, passed)
                for s in range(SUB):
                    ins = dve.bn_aggr(mv[:, s, :], stats[:, s, :])
                ins.then_inc(var_done, 1)
                dve.wait_ge(std_done, T + 1)
                dve.reciprocal(rstd[:, :], std[:, :]).then_inc(rstd_done, 1)
                dve.wait_ge(rstd_done, T + 1)
                for s in range(SUB):
                    ins = dve.tensor_scalar(xn[:, s, :], xin[:, u, s, :], mv[:, s, 0:1], rstd[:, s:s + 1],
                                            ALU.subtract, ALU.mult)
                ins.then_inc(xn_done, 1)

            def xt_rest(T, u, kt):
                dve.wait_ge(xt_hi_done, 4 * T + kt + 1)
                dve.tensor_tensor(xt_lo[:, u, kt, :], tr_ps[kt % 2][:, :], xt_hi[:, u, kt, :].bitcast(F32),
                                  ALU.subtract).then_inc(xt_lo_done, 1)

            def gates(T):
                count = [0]

                def after(ins):
                    count[0] += 1
                    ins.then_inc(link, 1)
                    dve.wait_ge(link, LINKS * T + count[0])

                def wide(a):
                    return a[:, :].unsqueeze(2).to_broadcast([P, SUB, E])

                other = prob[:, :, :].unsqueeze(2).to_broadcast([P, SUB, E, E])
                own = prob[:, :, :].unsqueeze(3).to_broadcast([P, SUB, E, E])
                dve.wait_ge(router_done, T + 1)
                after(dve.tensor_tensor(logit[:, :, :], lg_ps[:, 0:SUB * E].rearrange("p (s e) -> p s e", e=E),
                                        r_bias[:, :].unsqueeze(1).to_broadcast([P, SUB, E]), ALU.add))
                after(dve.tensor_reduce(top[:, :], logit[:, :, :], AX.X, ALU.max))
                dve.tensor_tensor(shifted[:, :, :], logit[:, :, :], wide(top), ALU.subtract).then_inc(shift_done, 1)
                dve.wait_ge(ex_done, T + 1)
                after(dve.tensor_reduce(den[:, :], ex[:, :, :], AX.X, ALU.add))
                after(dve.reciprocal(rden[:, :], den[:, :]))
                after(dve.tensor_tensor(prob[:, :, :], ex[:, :, :], wide(rden), ALU.mult))
                after(dve.tensor_tensor(above[:, :, :, :], other, own, ALU.is_gt))
                after(dve.tensor_tensor(ties[:, :, :, :], other, own, ALU.is_equal))
                after(dve.tensor_tensor(ties[:, :, :, :], ties[:, :, :, :],
                                        lower[:, :, :].unsqueeze(1).to_broadcast([P, SUB, E, E]), ALU.mult))
                after(dve.tensor_tensor(above[:, :, :, :], above[:, :, :, :], ties[:, :, :, :], ALU.add))
                after(dve.tensor_reduce(rank[:, :, :], above[:, :, :, :], AX.X, ALU.add))
                after(dve.scalar_tensor_tensor(picked[:, :, :], rank[:, :, :], 1.5, prob[:, :, :], ALU.is_lt, ALU.mult))
                after(dve.tensor_reduce(psum2[:, :], picked[:, :, :], AX.X, ALU.add))
                after(dve.reciprocal(rpsum2[:, :], psum2[:, :]))
                after(dve.scalar_tensor_tensor(gate[:, :, :], picked[:, :, :], LORA_SCALING, wide(rpsum2), ALU.mult, ALU.mult))
                assert count[0] == LINKS
                dve.wait_ge(mid_done, T + 1)
                gate_r = gate[:, :, :].rearrange("p s e -> p (s e)").unsqueeze(2).to_broadcast([P, SUB * E, RANK])
                dve.tensor_tensor(mid[:, :, :].rearrange("p s (e r) -> p (s e) r", r=RANK),
                                  mid_ps[:, :].rearrange("p (a r) -> p a r", r=RANK), gate_r, ALU.mult).then_inc(gated, 1)

            def mid_rest(T):
                dve.wait_ge(mt_hi_done, T + 1)
                dve.tensor_tensor(mt_lo[:, :], mid_ps[:, :], mt_hi[:, :].bitcast(F32), ALU.subtract).then_inc(mt_lo_done, 1)

            def final(T, i, u, s):
                dve.wait_ge(out_done, 4 * T + s + 1 + START)
                if s == 0:
                    dve.wait_ge(biased, T + 1)
                    dve.wait_ge(y_stored[u], 16 * i + START)
                dve.tensor_tensor(y[:, u, s, :], out_ps[s % 2][:, :], xin[:, u, s, :], ALU.add).then_inc(y_done, 1)

            def tile(T, i, u, more, load):
                gates(T)
                if load:
                    ctx_rest(T + 2, u)
                if more:
                    add_and_norm(T + 1, i + u, 1 - u)
                mid_rest(T)
                final(T, i, u, 0)
                final(T, i, u, 1)
                if more:
                    xt_rest(T + 1, 1 - u, 0)
                    xt_rest(T + 1, 1 - u, 1)
                final(T, i, u, 2)
                if more:
                    xt_rest(T + 1, 1 - u, 2)
                    xt_rest(T + 1, 1 - u, 3)
                final(T, i, u, 3)

            dve.sem_inc(added, AHEAD)
            dve.sem_inc(y_done, FREE)
            dve.wait_ge(consts_done, 2)
            dve.wait_ge(bias_loaded, 32)
            ctx_rest(0, 0)
            ctx_rest(1, 1)
            add_and_norm(0, 0, 0)
            for kt in range(KT):
                xt_rest(0, 0, kt)
            with dve.Fori(0, TILES // 2 - 1) as i:
                for u in range(2):
                    tile(2 * i + u, i, u, True, True)
            tile(TILES - 2, TILES // 2 - 1, 0, True, False)
            tile(TILES - 1, TILES // 2 - 1, 1, False, False)


def layer(nc, x, wq_t, wk_t, wv_t, wo_t, rope, base_t, base_b, router_t, router_b, lora_a, lora_b, out):
    qk_scr = nc.dram_tensor("qk_scratch", [4, GROUPS, P, SEQ], F32, kind="Internal").ap()
    v_scr = nc.dram_tensor("v_scratch", [GROUPS, SEQ, P], F32, kind="Internal").ap()
    ctx_scr = nc.dram_tensor("ctx_scratch", [GROUPS, P, SEQ], F32, kind="Internal").ap()
    project(nc, x, wq_t, wk_t, wv_t, rope, qk_scr, v_scr)
    attend(nc, qk_scr, v_scr, ctx_scr)
    finish(nc, x, ctx_scr, wo_t, base_t, base_b, router_t, router_b, lora_a, lora_b, out)


def rope_tables():
    inv = np.exp(np.float32(-np.log(THETA)) * np.arange(0, DK, 2, dtype=np.float32) / np.float32(DK)).astype(np.float32)
    angle = (np.arange(SEQ, dtype=np.float32)[None, :] * inv[:, None]).astype(np.float32).astype(np.float64)
    one = np.stack([-np.sin(angle), np.cos(angle), np.sin(angle)], axis=1).astype(np.float32)
    return np.ascontiguousarray(np.tile(one, (P // (DK // 2), 1, BATCH)))


def kernel(L0_attn_x, L0_attn_Wq, L0_attn_Wk, L0_attn_Wv, L0_attn_Wo, L0_ffn_base_w, L0_ffn_base_b,
           L0_ffn_router_w, L0_ffn_router_b, L0_ffn_lora_A, L0_ffn_lora_B):
    import concourse.bacc as bacc
    from concourse.bass_utils import run_bass_kernel_spmd

    def turned(w):
        return np.ascontiguousarray(np.transpose(np.asarray(w)))

    def halves(w):
        return np.ascontiguousarray(np.asarray(w).reshape(2, 8, DK // 2, 2, DM).transpose(4, 0, 3, 1, 2).reshape(DM, DM))

    arrays = {
        "x": np.asarray(L0_attn_x).reshape(TOKENS, DM),
        "wq_t": halves(L0_attn_Wq),
        "wk_t": halves(L0_attn_Wk),
        "wv_t": turned(L0_attn_Wv),
        "wo_t": turned(L0_attn_Wo),
        "rope": rope_tables(),
        "base_t": turned(L0_ffn_base_w),
        "base_b": np.asarray(L0_ffn_base_b).reshape(1, DM),
        "router_t": turned(L0_ffn_router_w),
        "router_b": np.asarray(L0_ffn_router_b).reshape(1, EXPERTS),
        "lora_a": np.ascontiguousarray(np.asarray(L0_ffn_lora_A).transpose(1, 0, 2).reshape(DM, EXPERTS * RANK)),
        "lora_b": np.asarray(L0_ffn_lora_B).reshape(EXPERTS * RANK, DM),
    }
    nc = bacc.Bacc("TRN2", target_bir_lowering=False, num_devices=1)
    args = [nc.dram_tensor(f"in_{name}", a.shape, F32, kind="ExternalInput").ap() for name, a in arrays.items()]
    out = nc.dram_tensor("out", [TOKENS, DM], F32, kind="ExternalOutput").ap()
    nc.disable_value_cache = True
    layer(nc, *args, out)
    r = run_bass_kernel_spmd(nc, [{f"in_{name}": a for name, a in arrays.items()}], core_ids=[0])
    return r.results[0]["out"].reshape(BATCH, SEQ, DM)
```

```python
from contextlib import ExitStack

import numpy as np

import concourse.bass as bass
from concourse import mybir

F32 = mybir.dt.float32
F32R = mybir.dt.float32r
BF16 = mybir.dt.bfloat16
ALU = mybir.AluOpType
ACT = mybir.ActivationFunctionType
AX = mybir.AxisListType

P = 128
BATCH, SEQ, DM = 2, 2048, 512
HEADS, DK = 16, 32
EXPERTS, RANK = 8, 16
TOKENS = BATCH * SEQ
KT = DM // P
TT = 512
TILES = TOKENS // TT
SUB = TT // P
HG = 4
GROUPS = BATCH * HEADS // HG
QT = SEQ // TT
KB = SEQ // P
EPS = 1e-5
THETA = 10000.0
LORA_SCALING = 2.0
SCORE_SCALE = 1.0 / float(np.sqrt(DK))
MASKED = -1e38
W_RING = 4
START = 1

STEPS = [(t, j) for t in range(QT) for j in range((t + 1) * SUB)]
NSTEP = len(STEPS)
UNIT_END = [STEPS.index((t, (t + 1) * SUB - 1)) for t in range(QT)]
NPAIR = NSTEP // 2
LAG = 2
RING = 5
ITEMS = [(t, qi, h, c) for t in range(QT) for qi in range(SUB) for h in range(HG) for c in range(t + 1)]
NITEM = len(ITEMS)
ITEM_END = [max(n for n, it in enumerate(ITEMS) if it[0] == t) for t in range(QT)]
LEAD = 20
PER = NITEM // NSTEP
PER_FIRST = 6
BEFORE_FIRST = ITEM_END[1] + 1


def items_before(s, first):
    return min(BEFORE_FIRST + PER_FIRST * s, PER * (s + LEAD)) if first else PER * (s + LEAD)


def items_of_step(s, first):
    return [(f // NITEM, f % NITEM) for f in range(items_before(s, first), items_before(s + 1, first))]


def unit_ended_before(s, steps):
    e = s - steps
    return [(int(e < 0), t) for t in range(QT) if UNIT_END[t] == e % NSTEP]


def wait_alone(eng, semaphore, value, passed):
    eng.wait_ge(semaphore, value)
    eng.sem_inc(passed, 1)


def units_ended_at_step(s, first):
    return [(n, ITEMS[k][0]) for n, k in items_of_step(s, first) if k in ITEM_END]


class Weights:

    def __init__(self, jobs, raw, loaded, hi_done, lo_done):
        self.jobs, self.raw, self.loaded, self.hi_done, self.lo_done = jobs, raw, loaded, hi_done, lo_done

    def staging(self, n):
        return self.raw[:, n % len(self.loaded), 0:self.jobs[n][0].shape[-1]]

    def load(self, eng, n):
        ring = len(self.loaded)
        if n >= ring:
            eng.wait_ge(self.lo_done, n - ring + 1)
        eng.dma_start(self.staging(n), self.jobs[n][0]).then_inc(self.loaded[n % ring], 16)

    def round(self, act, n):
        ring = len(self.loaded)
        act.wait_ge(self.loaded[n % ring], 16 * (n // ring + 1))
        act.activation(self.jobs[n][1], self.staging(n), ACT.Copy).then_inc(self.hi_done, 1)

    def rest(self, dve, n):
        dve.wait_ge(self.hi_done, n + 1)
        dve.tensor_tensor(self.jobs[n][2], self.staging(n), self.jobs[n][1].bitcast(F32),
                          ALU.subtract).then_inc(self.lo_done, 1)


def project(nc, x, wq_t, wk_t, wv_t, rope, qk_scr, v_scr):
    x_v = x.rearrange("(t s p) d -> t p s d", p=P, s=SUB)
    rope_v = rope.rearrange("p c (t n) -> t p c n", n=TT)
    with ExitStack() as ctx:
        def sb(name, shape, dt=F32):
            return ctx.enter_context(nc.sbuf_tensor(name, shape, dt))

        def sem(name):
            return ctx.enter_context(nc.semaphore(name))

        w_raw = sb("p_w_raw", [P, W_RING, DM])
        w_hi = sb("p_w_hi", [P, KT, 3 * DM], F32R)
        w_lo = sb("p_w_lo", [P, KT, 3 * DM], F32R)
        ident = sb("p_ident", [P, P])
        xb = sb("p_x", [P, 2, SUB, DM])
        stats = sb("p_stats", [P, SUB, 6])
        mv = sb("p_mv", [P, SUB, 2])
        std = sb("p_std", [P, SUB])
        rstd = sb("p_rstd", [P, SUB])
        xt_hi = sb("p_xt_hi", [P, 2, KT, TT], F32R)
        xt_lo = sb("p_xt_lo", [P, 2, KT, TT], F32R)
        tab = sb("p_tab", [P, 2, 3, TT])
        mul = sb("p_mul", [P, 2, 2, 2, TT])
        rot = sb("p_rot", [P, 2, 2, TT])
        rot_hi = sb("p_rot_hi", [P, 2, 2, TT], F32R)
        rot_lo = sb("p_rot_lo", [P, 2, 2, TT], F32R)
        v_st = sb("p_v_st", [P, 2, SUB, DM])
        pair_ps = [ctx.enter_context(nc.psum_tensor(f"p_pair{n}", [P, 2, TT], F32)) for n in range(2)]
        tr_ps = [ctx.enter_context(nc.psum_tensor(f"p_tr{n}", [P, TT], F32)) for n in range(2)]
        v_ps = [ctx.enter_context(nc.psum_tensor(f"p_v{n}", [P, DM], F32)) for n in range(2)]

        w_loaded = [sem(f"p_w_loaded{n}") for n in range(W_RING)]
        w_hi_done, w_lo_done = sem("p_w_hi_done"), sem("p_w_lo_done")
        zeroed, ident_done = sem("p_zeroed"), sem("p_ident_done")
        x_loaded = [sem("p_x_loaded0"), sem("p_x_loaded1")]
        tab_loaded = [sem("p_tab_loaded0"), sem("p_tab_loaded1")]
        stats_done, var_done, std_done = sem("p_stats_done"), sem("p_var_done"), sem("p_std_done")
        passed = sem("p_passed")
        rstd_done, xn_done = sem("p_rstd_done"), sem("p_xn_done")
        tr_done, xt_hi_done, xt_lo_done = sem("p_tr_done"), sem("p_xt_hi_done"), sem("p_xt_lo_done")
        pair_done, v_done, v_copied = sem("p_pair_done"), sem("p_v_done"), sem("p_v_copied")
        mul_done, rot_done = sem("p_mul_done"), sem("p_rot_done")
        rot_hi_done, rot_lo_done = sem("p_rot_hi_done"), sem("p_rot_lo_done")
        rot_stored = [sem("p_rot_stored0"), sem("p_rot_stored1")]
        v_stored = [sem("p_v_stored0"), sem("p_v_stored1")]
        AHEAD = 2

        block = ctx.enter_context(nc.Block())
        jobs = [(w[kt * P:(kt + 1) * P, :], w_hi[:, kt, n * DM:(n + 1) * DM], w_lo[:, kt, n * DM:(n + 1) * DM])
                for n, w in enumerate((wq_t, wk_t, wv_t)) for kt in range(KT)]

        weights = Weights(jobs, w_raw, w_loaded, w_hi_done, w_lo_done)

        @block.gpsimd
        def _(pool):
            for semaphore in (v_done, *rot_stored, *v_stored):
                pool.sem_inc(semaphore, START)
            pool.memset(ident[:, :], 0.0).then_inc(zeroed, 1)
            pool.wait_ge(zeroed, 1)
            pool.affine_select(ident[:, :], ident[:, :], pattern=[[-1, P]], compare_op=ALU.not_equal,
                               fill=1.0, base=0, channel_multiplier=1).then_inc(ident_done, 1)

            def rope_sum(m, par):
                pool.wait_ge(mul_done, m + 1 + AHEAD)
                pool.wait_ge(rot_lo_done, m + 1)
                pool.tensor_tensor(rot[:, par], mul[:, par, :, 0, :], mul[:, par, :, 1, :],
                                   ALU.add).then_inc(rot_done, 1)

            pool.sem_inc(rot_done, AHEAD)
            with pool.Fori(0, TILES) as T:
                for p in range(4):
                    rope_sum(4 * T + p, p % 2)

        @block.sync
        def _(sp):
            for s in range(SUB):
                sp.dma_start(xb[:, 0, s], x_v[0][:, s]).then_inc(x_loaded[0], 16)
            for n in range(2 * KT):
                weights.load(sp, n)
            sp.dma_start(tab[:, 0], rope_v[0]).then_inc(tab_loaded[0], 16)
            for n in range(2 * KT, len(jobs)):
                weights.load(sp, n)
            sp.dma_start(xb[:, 1], x_v[1]).then_inc(x_loaded[1], 16)
            sp.dma_start(tab[:, 1], rope_v[1]).then_inc(tab_loaded[1], 16)
            with sp.Fori(0, BATCH) as b:
                with sp.Fori(0, 2) as half:
                    for u in range(2):
                        T = 4 * b + 2 * half + u
                        tok = bass.ds(1024 * half + 512 * u, TT)
                        for p in range(4):
                            m = 4 * T + p
                            rows = bass.ds(512 * b + 256 * (p % 2), 256)
                            sp.wait_ge(rot_lo_done, m + 1 + AHEAD)
                            for n, src in enumerate((rot_hi, rot_lo)):
                                dst = qk_scr[2 * (p // 2) + n].rearrange("g r n -> (g r) n")[rows, tok]
                                sp.dma_start(dst.rearrange("(p a) n -> p a n", a=2),
                                             src[:, p % 2].bitcast(F32)).then_inc(rot_stored[p % 2], 16)
                        sp.wait_ge(v_copied, 4 * T + 4 + AHEAD)
                        for hg in range(4):
                            dst = v_scr[4 * b + hg][tok, :].rearrange("(s p) c -> p s c", p=P)
                            sp.dma_start(dst, v_st[:, u, :, hg * P:(hg + 1) * P]).then_inc(v_stored[u], 16)
            for u in range(2):
                sp.wait_ge(rot_stored[u], 32 * 2 * TILES + START)
                sp.wait_ge(v_stored[u], 64 * TILES // 2 + START)

        @block.tensor
        def _(pe):
            pe.wait_ge(ident_done, 1)

            def transposes(T, u):
                pe.wait_ge(xn_done, T + 1)
                for kt in range(KT):
                    if isinstance(T, int) and 4 * T + kt - 1 <= 0:
                        pass
                    else:
                        pe.wait_ge(xt_lo_done, 4 * T + kt - 1)
                    for s in range(SUB):
                        mm = pe.transpose(tr_ps[kt % 2][:, s * P:(s + 1) * P],
                                          xb[:, u, s, kt * P:(kt + 1) * P], ident[:, :])
                    mm.then_inc(tr_done, 1)

            def qk_pair(T, u, p):
                pe.wait_ge(mul_done, 4 * T + p + 1)
                for half in range(2):
                    cols = slice((2 * p + half) * P, (2 * p + half + 1) * P)
                    passes = [(w, a, kt) for w, a in ((w_hi, xt_hi), (w_lo, xt_hi), (w_hi, xt_lo)) for kt in range(KT)]
                    for n, (w, a, kt) in enumerate(passes):
                        mm = pe.matmul(pair_ps[p % 2][:, half, :], w[:, kt, cols], a[:, u, kt, :],
                                       start=(n == 0), stop=(n == len(passes) - 1))
                mm.then_inc(pair_done, 1)

            def v_sub(T, u, s):
                pe.wait_ge(v_copied, 4 * T + s + 1)
                passes = [(a, w, kt) for a, w in ((xt_hi, w_hi), (xt_hi, w_lo), (xt_lo, w_hi)) for kt in range(KT)]
                for n, (a, w, kt) in enumerate(passes):
                    mm = pe.matmul(v_ps[s % 2][:, :], a[:, u, kt, s * P:(s + 1) * P], w[:, kt, 2 * DM:3 * DM],
                                   start=(n == 0), stop=(n == len(passes) - 1))
                mm.then_inc(v_done, 1)

            def tile(T, u, more):
                pe.wait_ge(xt_lo_done, 4 * T + 4)
                for p in range(4):
                    qk_pair(T, u, p)
                    v_sub(T, u, p)
                    if p == 1 and more:
                        transposes(T + 1, 1 - u)

            transposes(0, 0)
            pe.wait_ge(w_lo_done, len(jobs))
            with pe.Fori(0, TILES // 2 - 1) as i:
                for u in range(2):
                    tile(2 * i + u, u, True)
            tile(TILES - 2, 0, True)
            tile(TILES - 1, 1, False)

        @block.scalar
        def _(act):
            def load_x(T, u):
                act.dma_start(xb[:, u], x_v[T]).then_inc(x_loaded[u], 16)

            def load_tab(T, u):
                act.dma_start(tab[:, u], rope_v[T]).then_inc(tab_loaded[u], 16)

            def root(T):
                act.wait_ge(var_done, T + 1)
                act.activation(std[:, :], mv[:, :, 1], ACT.Sqrt, bias=EPS).then_inc(std_done, 1)

            def xt_copy(T, u, kt):
                act.wait_ge(tr_done, 4 * T + kt + 1)
                act.activation(xt_hi[:, u, kt, :], tr_ps[kt % 2][:, :], ACT.Copy).then_inc(xt_hi_done, 1)

            def rot_copy(T, i, p):
                act.wait_ge(rot_done, 4 * T + p + 1 + AHEAD)
                act.wait_ge(rot_stored[p % 2], 32 * (2 * T + p // 2) + START)
                act.activation(rot_hi[:, p % 2], rot[:, p % 2], ACT.Copy).then_inc(rot_hi_done, 1)

            def v_copy(T, i, u, s):
                act.wait_ge(v_done, 4 * T + s + 1 + START)
                if s == 0:
                    act.wait_ge(v_stored[u], 64 * i + START)
                act.activation(v_st[:, u, s, :], v_ps[s % 2][:, :], ACT.Copy).then_inc(v_copied, 1)

            def tile(T, i, u, more, load):
                if load:
                    load_x(T + 2, u)
                if more:
                    root(T + 1)
                v_copy(T, i, u, 0)
                rot_copy(T, i, 0)
                v_copy(T, i, u, 1)
                if more:
                    act.wait_ge(v_done, 4 * T + START)
                    for kt in range(KT):
                        xt_copy(T + 1, 1 - u, kt)
                rot_copy(T, i, 1)
                v_copy(T, i, u, 2)
                rot_copy(T, i, 2)
                v_copy(T, i, u, 3)
                rot_copy(T, i, 3)
                if load:
                    act.wait_ge(mul_done, 4 * T + 4 + AHEAD)
                    load_tab(T + 2, u)

            for n in range(KT):
                weights.round(act, n)
            root(0)
            for kt in range(KT):
                xt_copy(0, 0, kt)
            for n in range(KT, len(jobs)):
                weights.round(act, n)
            act.sem_inc(v_copied, AHEAD)
            with act.Fori(0, TILES // 2 - 1) as i:
                for u in range(2):
                    tile(2 * i + u, i, u, True, True)
            tile(TILES - 2, TILES // 2 - 1, 0, True, False)
            tile(TILES - 1, TILES // 2 - 1, 1, False, False)

        @block.vector
        def _(dve):
            def layer_norm(T, i, u):
                if isinstance(T, int) and T == 0:
                    dve.wait_ge(x_loaded[0], 16 * SUB)
                else:
                    dve.wait_ge(x_loaded[u], 16 * i + (16 * SUB if u == 0 else 16))
                if not (isinstance(T, int) and T == 0):
                    dve.wait_ge(xn_done, T)
                for s in range(SUB):
                    ins = dve.bn_stats(stats[:, s, :], xb[:, u, s, :])
                ins.then_inc(stats_done, 1)
                wait_alone(dve, stats_done, T + 1, passed)
                for s in range(SUB):
                    ins = dve.bn_aggr(mv[:, s, :], stats[:, s, :])
                ins.then_inc(var_done, 1)
                dve.wait_ge(std_done, T + 1)
                dve.reciprocal(rstd[:, :], std[:, :]).then_inc(rstd_done, 1)
                dve.wait_ge(rstd_done, T + 1)
                for s in range(SUB):
                    ins = dve.tensor_scalar(xb[:, u, s, :], xb[:, u, s, :], mv[:, s, 0:1], rstd[:, s:s + 1],
                                            ALU.subtract, ALU.mult)
                ins.then_inc(xn_done, 1)

            def xt_rest(T, u, kt):
                dve.wait_ge(xt_hi_done, 4 * T + kt + 1)
                dve.tensor_tensor(xt_lo[:, u, kt, :], tr_ps[kt % 2][:, :], xt_hi[:, u, kt, :].bitcast(F32),
                                  ALU.subtract).then_inc(xt_lo_done, 1)

            def rope_mul(T, i, u, p):
                if p == 0:
                    dve.wait_ge(tab_loaded[u], 16 * i + 16)
                dve.wait_ge(pair_done, 4 * T + p + 1)
                dve.wait_ge(rot_done, 4 * T + p + 1)
                even, odd = (pair_ps[p % 2][:, n:n + 1, :].to_broadcast([P, 2, TT]) for n in range(2))
                dve.tensor_tensor(mul[:, p % 2, :, 0, :], even, tab[:, u, 1:3, :], ALU.mult)
                dve.tensor_tensor(mul[:, p % 2, :, 1, :], odd, tab[:, u, 0:2, :], ALU.mult).then_inc(mul_done, 1)

            def rot_rest(T, p):
                dve.wait_ge(rot_hi_done, 4 * T + p + 1)
                dve.tensor_tensor(rot_lo[:, p % 2], rot[:, p % 2], rot_hi[:, p % 2].bitcast(F32),
                                  ALU.subtract).then_inc(rot_lo_done, 1)

            def tile(T, i, u, more):
                if more:
                    layer_norm(T + 1, i + u, 1 - u)
                rope_mul(T, i, u, 0)
                rope_mul(T, i, u, 1)
                rot_rest(T, 0)
                if more:
                    for kt in range(KT):
                        xt_rest(T + 1, 1 - u, kt)
                rope_mul(T, i, u, 2)
                rot_rest(T, 1)
                rope_mul(T, i, u, 3)
                rot_rest(T, 2)
                rot_rest(T, 3)

            dve.sem_inc(mul_done, AHEAD)
            dve.sem_inc(rot_lo_done, AHEAD)
            layer_norm(0, 0, 0)
            for n in range(KT):
                weights.rest(dve, n)
            for kt in range(KT):
                xt_rest(0, 0, kt)
            for n in range(KT, len(jobs)):
                weights.rest(dve, n)
            with dve.Fori(0, TILES // 2 - 1) as i:
                for u in range(2):
                    tile(2 * i + u, i, u, True)
            tile(TILES - 2, TILES // 2 - 1, 0, True)
            tile(TILES - 1, TILES // 2 - 1, 1, False)


def attend(nc, qk_scr, v_scr, ctx_scr):
    with ExitStack() as ctx:
        def sb(name, shape, dt=F32):
            return ctx.enter_context(nc.sbuf_tensor(name, shape, dt))

        def sem(name):
            return ctx.enter_context(nc.semaphore(name))

        q_stack = sb("a_q_stack", [P, HG, SEQ], F32R)
        k_stack = [sb(f"a_k_stack{n}", [P, HG, SEQ], F32R) for n in range(2)]
        vb = sb("a_v", [P, 2, KB, P])
        probs = sb("a_probs", [P, RING, HG, TT])
        pair = sb("a_pair", [P, 2, HG, TT])
        ctx_st = sb("a_ctx_st", [P, 2, TT])
        sum_t = sb("a_sum_t", [P, TT])
        rsum = sb("a_rsum", [P, TT // 32])
        rsum_b = sb("a_rsum_b", [P, TT])
        mask = sb("a_mask", [P, TT])
        ones = sb("a_ones", [P, DK])
        ident = sb("a_ident", [P, P])
        eye = sb("a_eye", [P, P], BF16)
        later = sb("a_later", [P, P], BF16)
        part = sb("a_part", [P, HG * SUB, QT])
        neg_max = sb("a_neg_max", [P, HG * SUB])
        neg_parts = sb("a_neg_parts", [P, HG, 2, SUB])
        neg_rows = sb("a_neg_rows", [2 * HG * SUB, 2, P])
        st_ps = ctx.enter_context(nc.psum_tensor("a_st", [P, HG, TT], F32))
        mx_ps = [ctx.enter_context(nc.psum_tensor(f"a_mx{n}", [P, TT], F32)) for n in range(2)]
        av_ps = ctx.enter_context(nc.psum_tensor("a_av", [P, TT], F32))
        sum_ps = ctx.enter_context(nc.psum_tensor("a_sum", [P, TT], F32))

        kv_loaded = [sem("a_kv_loaded0"), sem("a_kv_loaded1")]
        q_loaded = [sem(f"a_q_loaded{t}") for t in range(QT)]
        shift_loaded = [sem("a_shift_loaded0"), sem("a_shift_loaded1")]
        consts_done, zeroed = sem("a_consts_done"), sem("a_zeroed")
        mask_done, key_ones, ones_done = sem("a_mask_done"), sem("a_key_ones"), sem("a_ones_done")
        st_done, exp_done, step_done = sem("a_st_done"), sem("a_exp_done"), sem("a_step_done")
        pair_added, pair_done = sem("a_pair_added"), sem("a_pair_done")
        av_copied, sum_turned = sem("a_av_copied"), sem("a_sum_turned")
        item_done, max_done = sem("a_item_done"), sem("a_max_done")
        dve_passed, reduced, rounded = sem("a_dve_passed"), sem("a_reduced"), sem("a_rounded")
        rsum_done, rsum_turned, out_done = sem("a_rsum_done"), sem("a_rsum_turned"), sem("a_out_done")
        neg_done, neg_turned, rows_done = sem("a_neg_done"), sem("a_neg_turned"), sem("a_rows_done")
        ctx_stored = [sem("a_ctx_stored0"), sem("a_ctx_stored1")]
        KV_LOADS, Q_LOADS, SHIFTS = 16 * 5, 16 * 3, 16 * HG
        AHEAD = 2
        BANKS = HG
        FREE = (RING + 1) // 2

        block = ctx.enter_context(nc.Block())

        def exps(g, s, h):
            return HG * NSTEP * g + HG * s + h + 1 + BANKS

        def pairs(g, p):
            return NPAIR * g + p + 1 + FREE

        @block.sync
        def _(sp):
            def load_kv(g, par):
                for n, kind in enumerate((2, 3, 2)):
                    sp.dma_start(k_stack[par][32 * n:32 * n + 32].bitcast(F32),
                                 qk_scr[kind, g].rearrange("(h r) n -> r h n", r=DK)).then_inc(kv_loaded[par], 16)
                v_rows = v_scr[g].rearrange("(a j p) c -> a p j c", p=P, a=2)
                for n in range(2):
                    sp.dma_start(vb[:, par, n * KB // 2:(n + 1) * KB // 2], v_rows[n]).then_inc(kv_loaded[par], 16)

            def load_q(g, t):
                for n, kind in enumerate((0, 0, 1)):
                    sp.dma_start(q_stack[32 * n:32 * n + 32, :, t * TT:(t + 1) * TT].bitcast(F32),
                                 qk_scr[kind, g].rearrange("(h r) n -> r h n", r=DK)[:, :, t * TT:(t + 1) * TT]
                                 ).then_inc(q_loaded[t], 16)

            def shift_rows(g, t):
                sp.wait_ge(rows_done, 4 * g + t + 1)
                for h in range(HG):
                    dst = q_stack[96:98, h, t * TT:(t + 1) * TT].bitcast(F32)
                    sp.dma_start(dst.rearrange("p (q c) -> p q c", c=P),
                                 neg_rows[8 * h:8 * h + 8, t % 2, :]).then_inc(shift_loaded[t % 2], 16)

            def store(g, t):
                sp.wait_ge(out_done, 4 * g + t + 1)
                sp.dma_start(ctx_scr[g][:, t * TT:(t + 1) * TT], ctx_st[:, t % 2]).then_inc(ctx_stored[t % 2], 16)

            def group(g, par, first, last):
                if not last:
                    if not first:
                        sp.wait_ge(step_done, NSTEP * g)
                    load_kv(g + 1, 1 - par)
                for s in range(NSTEP):
                    for nxt, t in units_ended_at_step(s, first):
                        if not (nxt and last):
                            shift_rows(g + nxt, t)
                    if s in UNIT_END and not last:
                        sp.wait_ge(st_done, HG * (NSTEP * g + s + 1))
                        load_q(g + 1, STEPS[s][0])
                    for before, t in unit_ended_before(s, LAG + 1):
                        if not (before and first):
                            store(g - before, t)

            load_q(0, 0)
            load_kv(0, 0)
            for t in range(1, QT):
                load_q(0, t)
            for t in range(QT):
                if ITEM_END[t] < BEFORE_FIRST:
                    shift_rows(0, t)
            group(0, 0, True, False)
            with sp.Fori(0, GROUPS // 2 - 1) as i:
                group(2 * i + 1, 1, False, False)
                group(2 * i + 2, 0, False, False)
            group(GROUPS - 1, 1, False, True)
            store(GROUPS - 1, QT - 1)
            for n in range(2):
                sp.wait_ge(ctx_stored[n], 16 * GROUPS * QT // 2 + START)

        @block.gpsimd
        def _(pool):
            for semaphore in (av_copied, sum_turned, neg_turned, *shift_loaded, *ctx_stored):
                pool.sem_inc(semaphore, START)
            for n, (buffer, value) in enumerate(((ident, 0.0), (eye, 0.0), (later, 0.0), (mask, 0.0))):
                pool.memset(buffer[:, :], value).then_inc(zeroed, 1)
                pool.wait_ge(zeroed, n + 1)
            pool.affine_select(mask[:, TT - P:TT], mask[:, TT - P:TT], pattern=[[-1, P]], compare_op=ALU.is_ge,
                               fill=MASKED, base=0, channel_multiplier=1).then_inc(mask_done, 1)
            for diagonal in (ident, eye):
                pool.affine_select(diagonal[:, :], diagonal[:, :], pattern=[[-1, P]], compare_op=ALU.not_equal,
                                   fill=1.0, base=0, channel_multiplier=1).then_inc(consts_done, 1)
            pool.affine_select(later[:, :], later[:, :], pattern=[[1, P]], compare_op=ALU.is_ge,
                               fill=MASKED, base=0, channel_multiplier=-1).then_inc(consts_done, 1)
            pool.wait_ge(consts_done, 3)
            for n in range(2):
                pool.memset(k_stack[n][96:98].bitcast(F32), 1.0).then_inc(key_ones, 1)
                pool.wait_ge(key_ones, n + 1)

            with pool.Fori(0, GROUPS) as g:
                for p in range(NPAIR):
                    s = 2 * p
                    t, j = STEPS[s]
                    q0 = max(0, j + 1 - t * SUB) * P
                    pool.wait_ge(pair_done, pairs(g, p - 2))
                    for h in range(0, HG, 2):
                        pool.wait_ge(exp_done, exps(g, s + 1, h + 1))
                        pool.tensor_tensor(pair[:, p % 2, h:h + 2, q0:TT], probs[:, s % RING, h:h + 2, q0:TT],
                                           probs[:, (s + 1) % RING, h:h + 2, q0:TT], ALU.add).then_inc(pair_added, 1)

        @block.tensor
        def _(pe):
            def item(g, par, use, k):
                t, qi, h, c = ITEMS[k]
                width = TT if c < t else (qi + 1) * P
                if k == 0:
                    pe.wait_ge(kv_loaded[par], KV_LOADS * use + KV_LOADS)
                if k == 0 or k - 1 in ITEM_END:
                    pe.wait_ge(q_loaded[t], Q_LOADS * g + Q_LOADS)
                pe.wait_ge(max_done, NITEM * g + k + 1)
                pe.matmul(mx_ps[k % 2][:, 0:width], q_stack[0:96, h, t * TT + qi * P:t * TT + (qi + 1) * P],
                          k_stack[par][0:96, h, c * TT:c * TT + width], start=True, stop=True).then_inc(item_done, 1)

            def turn_maxima(g, t, items):
                pe.wait_ge(neg_done, 4 * g + t + 1)
                pe.wait_ge(max_done, items - 1 + AHEAD)
                pe.transpose(mx_ps[0][0:2 * HG * SUB, 0:P], neg_parts[:, :, :, :].rearrange("p h n q -> p (h n q)"),
                             ident[:, :]).then_inc(neg_turned, 1)

            def scores(g, par, s, h):
                t, j = STEPS[s]
                diagonal = j >= t * SUB
                q0 = max(0, j - t * SUB) * P
                if j == 0 and h == 0:
                    pe.wait_ge(shift_loaded[t % 2], SHIFTS * (2 * g + t // 2 + 1) + START)
                pe.wait_ge(exp_done, HG * NSTEP * g + HG * s + h + 1)
                mm = pe.matmul(st_ps[:, h, q0:TT], k_stack[par][0:98, h, j * P:(j + 1) * P],
                               q_stack[0:98, h, t * TT + q0:(t + 1) * TT], start=True, stop=not diagonal)
                if diagonal:
                    mm = pe.matmul(st_ps[:, h, q0:q0 + P], eye[:, :], later[:, :], start=False, stop=True)
                mm.then_inc(st_done, 1)

            def values(g, par, s):
                t, j = STEPS[s]
                q0 = max(0, j - t * SUB) * P
                if j == 0:
                    pe.wait_ge(av_copied, 4 * g + t + START)
                for h in range(HG):
                    pe.wait_ge(exp_done, exps(g, s, h))
                    mm = pe.matmul(av_ps[h * DK:(h + 1) * DK, q0:TT], vb[:, par, j, h * DK:(h + 1) * DK],
                                   probs[:, s % RING, h, q0:TT], start=(j == 0), stop=s in UNIT_END,
                                   tile_position=(0, h * DK))
                mm.then_inc(step_done, 1)

            def sums(g, p):
                s = 2 * p
                t, j = STEPS[s]
                first, last = j == 0, s + 1 in UNIT_END
                q0 = max(0, j - t * SUB) * P
                q1 = max(0, j + 1 - t * SUB) * P
                if first:
                    pe.wait_ge(sum_turned, 4 * g + t + START)
                for h in range(HG):
                    rows = slice(h * DK, (h + 1) * DK)
                    if q1 > q0:
                        pe.matmul(sum_ps[rows, q0:q1], ones[:, :], probs[:, s % RING, h, q0:q1],
                                  start=first, stop=False, tile_position=(0, h * DK))
                for h in range(HG):
                    rows = slice(h * DK, (h + 1) * DK)
                    if h % 2 == 0:
                        pe.wait_ge(pair_added, 2 * (NPAIR * g + p) + h // 2 + 1)
                    mm = pe.matmul(sum_ps[rows, q1:TT], ones[:, :], pair[:, p % 2, h, q1:TT],
                                   start=first and q1 == q0, stop=last, tile_position=(0, h * DK))
                mm.then_inc(pair_done, 1)

            def group(g, par, use, first, last):
                next_use = use + par
                for s in range(NSTEP):
                    items = [(n, k) for n, k in items_of_step(s, first) if not (n and last)]
                    more = len(items) > PER
                    if items:
                        for n, t in units_ended_at_step(s - 2, first):
                            pe.wait_ge(rows_done, 4 * (g + n) + t + 1)

                    def next_item():
                        if items:
                            n, k = items.pop(0)
                            item(g + n, (par + n) % 2, next_use if n else use, k)

                    for half in range(2):
                        next_item()
                        for h in (2 * half, 2 * half + 1):
                            if s + 1 < NSTEP:
                                scores(g, par, s + 1, h)
                            elif not last:
                                scores(g + 1, 1 - par, 0, h)
                            if more and h == 0:
                                next_item()
                    next_item()
                    if (s - LAG) % 2 == 1 and not (s < LAG and first):
                        if s < LAG:
                            sums(g - 1, (s - LAG + NSTEP) // 2)
                        else:
                            sums(g, (s - LAG) // 2)
                        next_item()
                        values(g, par, s)
                    else:
                        values(g, par, s)
                        next_item()
                    if more:
                        next_item()
                    for n, t in units_ended_at_step(s - 1, first):
                        if not (n and last):
                            issued = items_before(s + 1, first)
                            turn_maxima(g + n, t, NITEM * g + (min(issued, NITEM) if last else issued))

            pe.wait_ge(consts_done, 3)
            for k in range(BEFORE_FIRST):
                item(0, 0, 0, k)
                for t in range(QT):
                    if k == ITEM_END[t] + PER:
                        turn_maxima(0, t, k + 1)
                        pe.wait_ge(rows_done, t + 1)
            pe.wait_ge(key_ones, 2)
            pe.wait_ge(ones_done, 1)
            for h in range(HG):
                scores(0, 0, 0, h)
            group(0, 0, 0, True, False)
            with pe.Fori(0, GROUPS // 2 - 1) as i:
                group(2 * i + 1, 1, i, False, False)
                group(2 * i + 2, 0, i + 1, False, False)
            group(GROUPS - 1, 1, GROUPS // 2 - 1, False, True)
            sums(GROUPS - 1, NPAIR - 1)

        @block.scalar
        def _(act):
            def copy_values(g, t):
                act.wait_ge(step_done, NSTEP * g + UNIT_END[t] + 1)
                act.wait_ge(ctx_stored[t % 2], 16 * (2 * g + t // 2) + START)
                act.activation(ctx_st[:, t % 2], av_ps[:, :], ACT.Copy).then_inc(av_copied, 1)

            def group(g, first):
                for s, (t, j) in enumerate(STEPS):
                    q0 = max(0, j - t * SUB) * P
                    act.wait_ge(pair_done, pairs(g, (s - RING) // 2))
                    for h in range(HG):
                        act.wait_ge(st_done, HG * NSTEP * g + HG * s + h + 1)
                        act.activation(probs[:, s % RING, h, q0:TT], st_ps[:, h, q0:TT], ACT.Exp,
                                       scale=SCORE_SCALE).then_inc(exp_done, 1)
                    for before, t_out in unit_ended_before(s, 1):
                        if not (before and first):
                            copy_values(g - before, t_out)

            act.sem_inc(exp_done, BANKS)
            group(0, True)
            with act.Fori(1, GROUPS) as g:
                group(g, False)
            copy_values(GROUPS - 1, QT - 1)

        @block.vector
        def _(dve):
            def item_max(g, k):
                t, qi, h, c = ITEMS[k]
                out = part[:, h * SUB + qi, c:c + 1]
                if c < t:
                    dve.wait_ge(item_done, NITEM * g + k + 1)
                    dve.tensor_reduce(out, mx_ps[k % 2][:, :], AX.X, ALU.max).then_inc(max_done, 1)
                else:
                    width = (qi + 1) * P
                    wait_alone(dve, item_done, NITEM * g + k + 1, dve_passed)
                    dve.tensor_tensor_reduce(out=mx_ps[k % 2][:, 0:width], in0=mx_ps[k % 2][:, 0:width],
                                             in1=mask[:, TT - width:TT], scale=1.0, scalar=3.0 * MASKED,
                                             op0=ALU.add, op1=ALU.max, accum_out=out).then_inc(max_done, 1)

            def unit_max(g, t, items):
                dve.wait_ge(max_done, items + AHEAD)
                dve.wait_ge(neg_turned, 4 * g + t + START)
                dve.tensor_reduce(neg_max[:, :], part[:, :, 0:t + 1], AX.X, ALU.max, negate=True).then_inc(reduced, 1)
                dve.wait_ge(reduced, 4 * g + t + 1)
                neg = neg_max[:, :].rearrange("p (h q) -> p h q", q=SUB)
                dve.tensor_copy(neg_parts[:, :, 0, :].bitcast(F32R), neg).then_inc(rounded, 1)
                dve.wait_ge(rounded, 4 * g + t + 1)
                dve.tensor_tensor(neg_parts[:, :, 1, :].bitcast(F32R), neg, neg_parts[:, :, 0, :],
                                  ALU.subtract).then_inc(neg_done, 1)

            def unit_rows(g, t):
                dve.wait_ge(neg_turned, 4 * g + t + 1 + START)
                dve.wait_ge(shift_loaded[t % 2], SHIFTS * (2 * g + t // 2) + START)
                dve.tensor_copy(neg_rows[:, t % 2, :].bitcast(F32R), mx_ps[0][0:32, 0:P]).then_inc(rows_done, 1)

            def turn_sums(g, t):
                dve.wait_ge(pair_done, pairs(g, UNIT_END[t] // 2))
                dve.transpose(sum_t[:, :], sum_ps[:, :]).then_inc(sum_turned, 1)

            def invert(g, t):
                dve.wait_ge(sum_turned, 4 * g + t + 1 + START)
                dve.reciprocal(rsum[:, :], sum_t[:, :].rearrange("p (b i) -> p b i", i=32)[:, :, 0]).then_inc(rsum_done, 1)

            def turn_back(g, t):
                dve.wait_ge(rsum_done, 4 * g + t + 1)
                dve.transpose(rsum_b[:, :], rsum[:, :].unsqueeze(2).to_broadcast([P, TT // 32, 32])).then_inc(rsum_turned, 1)

            def divide(g, t):
                dve.wait_ge(rsum_turned, 4 * g + t + 1)
                dve.wait_ge(av_copied, 4 * g + t + 1 + START)
                dve.tensor_tensor(ctx_st[:, t % 2], ctx_st[:, t % 2], rsum_b[:, :], ALU.mult).then_inc(out_done, 1)

            PARTS = ((turn_sums, LAG, 3), (invert, LAG + 1, 0), (turn_back, LAG + 1, 1), (divide, LAG + 1, 3))

            def group(g, first, last):
                for s in range(NSTEP):
                    for n, (nxt, k) in enumerate(items_of_step(s, first)):
                        if not (nxt and last):
                            item_max(g + nxt, k)
                        for part_of, steps, after in PARTS:
                            for before, t in unit_ended_before(s, steps):
                                if after == n and not (before and first):
                                    part_of(g - before, t)
                    for n, t in units_ended_at_step(s, first):
                        if not (n and last):
                            unit_max(g + n, t, NITEM * g + items_before(s + 1, first))
                    for n, t in units_ended_at_step(s - 1, first):
                        if not (n and last):
                            unit_rows(g + n, t)

            dve.memset(ones[:, :], 1.0).then_inc(ones_done, 1)
            dve.sem_inc(max_done, AHEAD)
            dve.sem_inc(pair_done, FREE)
            dve.wait_ge(mask_done, 1)
            for k in range(BEFORE_FIRST):
                item_max(0, k)
                for t in range(QT):
                    if k == ITEM_END[t]:
                        unit_max(0, t, k + 1)
                    if k == ITEM_END[t] + PER:
                        unit_rows(0, t)
            group(0, True, False)
            with dve.Fori(1, GROUPS - 1) as g:
                group(g, False, False)
            group(GROUPS - 1, False, True)
            for part_of, _, _ in PARTS:
                part_of(GROUPS - 1, QT - 1)


def finish(nc, x, ctx_scr, wo_t, base_t, base_b, router_t, router_b, lora_a, lora_b, out):
    x_v = x.rearrange("(t s p) d -> t p s d", p=P, s=SUB)
    out_v = out.rearrange("(t s p) d -> t p s d", p=P, s=SUB)
    ctx_v = ctx_scr.rearrange("(b k) p n -> b p k n", k=KT)
    E = EXPERTS
    with ExitStack() as ctx:
        def sb(name, shape, dt=F32):
            return ctx.enter_context(nc.sbuf_tensor(name, shape, dt))

        def sem(name):
            return ctx.enter_context(nc.semaphore(name))

        def psum(name, shape):
            return ctx.enter_context(nc.psum_tensor(name, shape, F32))

        w_raw = sb("f_w_raw", [P, W_RING, DM])
        wo_hi, wo_lo = sb("f_wo_hi", [P, KT, DM], F32R), sb("f_wo_lo", [P, KT, DM], F32R)
        base_hi, base_lo = sb("f_base_hi", [P, KT, DM], F32R), sb("f_base_lo", [P, KT, DM], F32R)
        a_hi, a_lo = sb("f_a_hi", [P, KT, P], F32R), sb("f_a_lo", [P, KT, P], F32R)
        r_hi, r_lo = sb("f_r_hi", [P, KT, E], F32R), sb("f_r_lo", [P, KT, E], F32R)
        b_hi, b_lo = sb("f_b_hi", [P, DM], F32R), sb("f_b_lo", [P, DM], F32R)
        bias = sb("f_bias", [P, DM])
        r_bias = sb("f_r_bias", [P, E])
        ident = sb("f_ident", [P, P])
        lower = sb("f_lower", [P, E, E])
        cin = sb("f_ctx", [P, KT, TT])
        c_hi, c_lo = sb("f_c_hi", [P, 2, KT, TT], F32R), sb("f_c_lo", [P, 2, KT, TT], F32R)
        xin = sb("f_x", [P, 2, SUB, DM])
        xn = sb("f_xn", [P, SUB, DM])
        xt_hi, xt_lo = sb("f_xt_hi", [P, 2, KT, TT], F32R), sb("f_xt_lo", [P, 2, KT, TT], F32R)
        stats, mv = sb("f_stats", [P, SUB, 6]), sb("f_mv", [P, SUB, 2])
        std, rstd = sb("f_std", [P, SUB]), sb("f_rstd", [P, SUB])
        logit, shifted, ex, prob = (sb(f"f_g{n}", [P, SUB, E]) for n in range(4))
        rank, picked, gate = (sb(f"f_h{n}", [P, SUB, E]) for n in range(3))
        top, den, rden, psum2, rpsum2 = (sb(f"f_s{n}", [P, SUB]) for n in range(5))
        above, ties = sb("f_above", [P, SUB, E, E]), sb("f_ties", [P, SUB, E, E])
        gate_x = sb("f_gate_x", [P, SUB, P])
        logit_t = sb("f_logit_t", [E, TT])
        mid = sb("f_mid", [P, TT])
        gated_mid = sb("f_gated_mid", [P, TT])
        mt_hi, mt_lo = sb("f_mt_hi", [P, TT], F32R), sb("f_mt_lo", [P, TT], F32R)
        y = sb("f_y", [P, 2, SUB, DM])
        wo_ps = [psum(f"f_wo_ps{n}", [P, DM]) for n in range(2)]
        tr_ps = [psum(f"f_tr_ps{n}", [P, TT]) for n in range(2)]
        out_ps = [psum(f"f_out_ps{n}", [P, DM]) for n in range(2)]
        mid_ps = psum("f_mid_ps", [P, TT])
        lg_ps = psum("f_lg_ps", [P, DM])

        w_loaded = [sem(f"f_w_loaded{n}") for n in range(W_RING)]
        w_hi_done, w_lo_done = sem("f_w_hi_done"), sem("f_w_lo_done")
        zeroed, consts_done, bias_loaded = sem("f_zeroed"), sem("f_consts_done"), sem("f_bias_loaded")
        ctx_loaded = sem("f_ctx_loaded")
        x_loaded = [sem("f_x_loaded0"), sem("f_x_loaded1")]
        c_hi_done, c_lo_done = sem("f_c_hi_done"), sem("f_c_lo_done")
        wo_done, added, stats_done, var_done = sem("f_wo_done"), sem("f_added"), sem("f_stats_done"), sem("f_var_done")
        std_done, rstd_done, xn_done, biased = sem("f_std_done"), sem("f_rstd_done"), sem("f_xn_done"), sem("f_biased")
        tr_done, xt_hi_done, xt_lo_done = sem("f_tr_done"), sem("f_xt_hi_done"), sem("f_xt_lo_done")
        router_done, mid_done, gated = sem("f_router_done"), sem("f_mid_done"), sem("f_gated")
        passed, pe_passed = sem("f_passed"), sem("f_pe_passed")
        logit_copied, logit_turned, mid_copied = sem("f_logit_copied"), sem("f_logit_turned"), sem("f_mid_copied")
        link, shift_done, ex_done = sem("f_link"), sem("f_shift_done"), sem("f_ex_done")
        gate_turned, mid_gated = sem("f_gate_turned"), sem("f_mid_gated")
        mt_hi_done, mt_lo_done = sem("f_mt_hi_done"), sem("f_mt_lo_done")
        out_done, y_done = sem("f_out_done"), sem("f_y_done")
        y_stored = [sem("f_y_stored0"), sem("f_y_stored1")]
        AHEAD = 2
        FREE = SUB + START

        block = ctx.enter_context(nc.Block())

        rows = [slice(kt * P, (kt + 1) * P) for kt in range(KT)]
        jobs = [(wo_t[rows[kt], :], wo_hi[:, kt, :], wo_lo[:, kt, :]) for kt in range(KT)]
        jobs += [(router_t[rows[kt], :], r_hi[:, kt, :], r_lo[:, kt, :]) for kt in range(KT)]
        jobs += [(lora_a[rows[kt], :], a_hi[:, kt, :], a_lo[:, kt, :]) for kt in range(KT)]
        jobs += [(base_t[rows[kt], :], base_hi[:, kt, :], base_lo[:, kt, :]) for kt in range(KT)]
        jobs += [(lora_b, b_hi[:, :], b_lo[:, :])]
        weights = Weights(jobs, w_raw, w_loaded, w_hi_done, w_lo_done)

        @block.sync
        def _(sp):
            for n in range(W_RING):
                weights.load(sp, n)
            sp.dma_start(bias[:, :], base_b.to_broadcast([P, DM])).then_inc(bias_loaded, 16)
            sp.dma_start(r_bias[:, :], router_b.to_broadcast([P, E])).then_inc(bias_loaded, 16)
            with sp.Fori(0, BATCH) as b:
                with sp.Fori(0, QT // 2) as half:
                    for u in range(2):
                        T = 4 * b + 2 * half + u
                        sp.wait_ge(c_lo_done, T + START)
                        sp.dma_start(cin[:, :, :], ctx_v[b, :, :, bass.ds(1024 * half + 512 * u, TT)]).then_inc(ctx_loaded, 16)
                        sp.wait_ge(y_done, 4 * T + START)
                        sp.dma_start(xin[:, u], x_v[T]).then_inc(x_loaded[u], 16)

        @block.gpsimd
        def _(pool):
            for semaphore in (c_lo_done, mid_copied, mid_gated, out_done, *y_stored):
                pool.sem_inc(semaphore, START)
            pool.memset(ident[:, :], 0.0).then_inc(zeroed, 1)
            pool.wait_ge(zeroed, 1)
            pool.memset(lower[:, :, :], 1.0).then_inc(zeroed, 1)
            pool.wait_ge(zeroed, 2)
            pool.affine_select(ident[:, :], ident[:, :], pattern=[[-1, P]], compare_op=ALU.not_equal,
                               fill=1.0, base=0, channel_multiplier=1).then_inc(consts_done, 1)
            pool.affine_select(lower[:, :, :], lower[:, :, :], pattern=[[1, E], [-1, E]], compare_op=ALU.is_gt,
                               fill=0.0, base=0, channel_multiplier=0).then_inc(consts_done, 1)
            pool.wait_ge(bias_loaded, 32)
            with pool.Fori(0, TILES // 2) as i:
                for u in range(2):
                    T = 2 * i + u
                    pool.wait_ge(xn_done, T + 1)
                    for s in range(SUB):
                        ins = pool.tensor_tensor(xin[:, u, s, :], xin[:, u, s, :], bias[:, :], ALU.add)
                    ins.then_inc(biased, 1)

        @block.tensor
        def _(pe):
            def product(out, pairs, done):
                for n, (w, a) in enumerate(pairs):
                    mm = pe.matmul(out, w, a, start=(n == 0), stop=(n == len(pairs) - 1))
                if done is not None:
                    mm.then_inc(done, 1)

            def attention_out(T, u, s):
                m = 4 * T + s
                if s == 0:
                    pe.wait_ge(c_lo_done, T + 1 + START)
                pe.wait_ge(added, m + 1)
                tok = slice(s * P, (s + 1) * P)
                product(wo_ps[s % 2][:, :], [(c[:, u, kt, tok], w[:, kt, :]) for c, w in
                        ((c_hi, wo_hi), (c_hi, wo_lo), (c_lo, wo_hi)) for kt in range(KT)], wo_done)

            def transposes(T, kt):
                if kt == 0:
                    pe.wait_ge(xn_done, T + 1)
                if not (isinstance(T, int) and 4 * T + kt - 1 <= 0):
                    pe.wait_ge(xt_lo_done, 4 * T + kt - 1)
                for s in range(SUB):
                    mm = pe.transpose(tr_ps[kt % 2][:, s * P:(s + 1) * P], xn[:, s, kt * P:(kt + 1) * P], ident[:, :])
                mm.then_inc(tr_done, 1)

            def router(T, u):
                pe.wait_ge(xt_lo_done, 4 * T + 4)
                pe.wait_ge(mid_gated, T + START)
                product(lg_ps[0:E, :], [(w[:, kt, :], a[:, u, kt, :]) for w, a in
                        ((r_hi, xt_hi), (r_lo, xt_hi), (r_hi, xt_lo)) for kt in range(KT)], router_done)

            def down(T, u):
                pe.wait_ge(mid_copied, T + START)
                product(mid_ps[:, :], [(w[:, kt, :], a[:, u, kt, :]) for w, a in
                        ((a_hi, xt_hi), (a_lo, xt_hi), (a_hi, xt_lo)) for kt in range(KT)], mid_done)

            def turn_logits(T):
                wait_alone(pe, logit_copied, T + 1, pe_passed)
                for s in range(SUB):
                    mm = pe.transpose(lg_ps[:, s * E:(s + 1) * E], logit_t[:, s * P:(s + 1) * P], ident[0:E, 0:E])
                mm.then_inc(logit_turned, 1)

            def base(T, u, s):
                pe.wait_ge(y_done, 4 * T + s - 1 + FREE)
                pairs = [(a[:, u, kt, s * P:(s + 1) * P], w[:, kt, :]) for a, w in
                         ((xt_hi, base_hi), (xt_hi, base_lo), (xt_lo, base_hi)) for kt in range(KT)]
                for n, (w, a) in enumerate(pairs):
                    pe.matmul(out_ps[s % 2][:, :], w, a, start=(n == 0), stop=False)

            def turn_gates(T):
                pe.wait_ge(gated, T + 1)
                for s in range(SUB):
                    mm = pe.transpose(lg_ps[:, s * P:(s + 1) * P], gate_x[:, s, :], ident[:, :])
                mm.then_inc(gate_turned, 1)

            def experts(T, s):
                pe.wait_ge(mt_lo_done, T + 1)
                tok = slice(s * P, (s + 1) * P)
                pairs = ((mt_hi, b_hi), (mt_hi, b_lo), (mt_lo, b_hi))
                for n, (a, w) in enumerate(pairs):
                    mm = pe.matmul(out_ps[s % 2][:, :], a[:, tok], w[:, :], start=False, stop=(n == len(pairs) - 1))
                mm.then_inc(out_done, 1)

            def tile(T, u, more):
                router(T, u)
                down(T, u)
                if more:
                    attention_out(T + 1, 1 - u, 0)
                turn_logits(T)
                if more:
                    attention_out(T + 1, 1 - u, 1)
                base(T, u, 0)
                base(T, u, 1)
                turn_gates(T)
                if more:
                    attention_out(T + 1, 1 - u, 2)
                    attention_out(T + 1, 1 - u, 3)
                experts(T, 0)
                experts(T, 1)
                base(T, u, 2)
                experts(T, 2)
                if more:
                    transposes(T + 1, 0)
                    transposes(T + 1, 1)
                base(T, u, 3)
                if more:
                    transposes(T + 1, 2)
                    transposes(T + 1, 3)
                experts(T, 3)

            pe.wait_ge(consts_done, 2)
            pe.wait_ge(w_lo_done, KT)
            for s in range(SUB):
                attention_out(0, 0, s)
            for kt in range(KT):
                transposes(0, kt)
            pe.wait_ge(w_lo_done, len(jobs))
            with pe.Fori(0, TILES // 2 - 1) as i:
                for u in range(2):
                    tile(2 * i + u, u, True)
            tile(TILES - 2, 0, True)
            tile(TILES - 1, 1, False)

        @block.scalar
        def _(act):
            def ctx_copy(T, u):
                act.wait_ge(ctx_loaded, 16 * T + 16)
                act.activation(c_hi[:, u], cin[:, :, :], ACT.Copy).then_inc(c_hi_done, 1)

            def root(T):
                act.wait_ge(var_done, T + 1)
                act.activation(std[:, :], mv[:, :, 1], ACT.Sqrt, bias=EPS).then_inc(std_done, 1)

            def xt_copy(T, u, kt):
                act.wait_ge(tr_done, 4 * T + kt + 1)
                act.activation(xt_hi[:, u, kt, :], tr_ps[kt % 2][:, :], ACT.Copy).then_inc(xt_hi_done, 1)

            def tile(T, u, more, load):
                act.wait_ge(router_done, T + 1)
                act.activation(logit_t[:, :], lg_ps[0:E, :], ACT.Copy).then_inc(logit_copied, 1)
                act.wait_ge(mid_done, T + 1)
                act.wait_ge(mid_gated, T + START)
                act.activation(mid[:, :], mid_ps[:, :], ACT.Copy).then_inc(mid_copied, 1)
                act.wait_ge(shift_done, T + 1)
                act.activation(ex[:, :, :], shifted[:, :, :], ACT.Exp).then_inc(ex_done, 1)
                act.wait_ge(mid_gated, T + 1 + START)
                act.wait_ge(out_done, 4 * T + START)
                act.activation(mt_hi[:, :], gated_mid[:, :], ACT.Copy).then_inc(mt_hi_done, 1)
                if more:
                    root(T + 1)
                    for kt in range(KT):
                        xt_copy(T + 1, 1 - u, kt)
                if load:
                    act.wait_ge(wo_done, 4 * T + 4)
                    ctx_copy(T + 2, u)
                act.wait_ge(y_done, 4 * T + 4 + FREE)
                act.dma_start(out_v[T], y[:, u]).then_inc(y_stored[u], 16)

            for n in range(len(jobs)):
                if n == KT:
                    ctx_copy(0, 0)
                weights.round(act, n)
                if n + W_RING < len(jobs):
                    weights.load(act, n + W_RING)
            ctx_copy(1, 1)
            root(0)
            for kt in range(KT):
                xt_copy(0, 0, kt)
            with act.Fori(0, TILES // 2 - 1) as i:
                for u in range(2):
                    tile(2 * i + u, u, True, True)
            tile(TILES - 2, 0, True, False)
            tile(TILES - 1, 1, False, False)
            for u in range(2):
                act.wait_ge(y_stored[u], 16 * TILES // 2 + START)

        @block.vector
        def _(dve):
            LINKS = 14

            def ctx_rest(T, u):
                dve.wait_ge(c_hi_done, T + 1)
                dve.tensor_tensor(c_lo[:, u], cin[:, :, :], c_hi[:, u].bitcast(F32), ALU.subtract).then_inc(c_lo_done, 1)

            def add(T, i, u, s):
                if s == 0:
                    dve.wait_ge(x_loaded[u], 16 * i + 16)
                dve.wait_ge(wo_done, 4 * T + s + 1)
                xs = xin[:, u, s, :]
                dve.tensor_tensor(xs, wo_ps[s % 2][:, :], xs, ALU.add).then_inc(added, 1)
                dve.wait_ge(added, 4 * T + s + 1 + AHEAD)
                dve.bn_stats(stats[:, s, :], xs).then_inc(stats_done, 1)

            def variances(T):
                wait_alone(dve, stats_done, 4 * T + 4, passed)
                for s in range(SUB):
                    ins = dve.bn_aggr(mv[:, s, :], stats[:, s, :])
                ins.then_inc(var_done, 1)

            def normalise(T, u):
                dve.wait_ge(std_done, T + 1)
                dve.reciprocal(rstd[:, :], std[:, :]).then_inc(rstd_done, 1)
                dve.wait_ge(rstd_done, T + 1)
                for s in range(SUB):
                    ins = dve.tensor_scalar(xn[:, s, :], xin[:, u, s, :], mv[:, s, 0:1], rstd[:, s:s + 1],
                                            ALU.subtract, ALU.mult)
                ins.then_inc(xn_done, 1)

            def xt_rest(T, u, kt):
                dve.wait_ge(xt_hi_done, 4 * T + kt + 1)
                dve.tensor_tensor(xt_lo[:, u, kt, :], tr_ps[kt % 2][:, :], xt_hi[:, u, kt, :].bitcast(F32),
                                  ALU.subtract).then_inc(xt_lo_done, 1)

            def gates(T):
                count = [0]

                def after(ins):
                    count[0] += 1
                    ins.then_inc(link, 1)
                    dve.wait_ge(link, LINKS * T + count[0])

                def wide(a):
                    return a[:, :].unsqueeze(2).to_broadcast([P, SUB, E])

                other = prob[:, :, :].unsqueeze(2).to_broadcast([P, SUB, E, E])
                own = prob[:, :, :].unsqueeze(3).to_broadcast([P, SUB, E, E])
                dve.wait_ge(logit_turned, T + 1)
                after(dve.tensor_tensor(logit[:, :, :], lg_ps[:, 0:SUB * E].rearrange("p (s e) -> p s e", e=E),
                                        r_bias[:, :].unsqueeze(1).to_broadcast([P, SUB, E]), ALU.add))
                after(dve.tensor_reduce(top[:, :], logit[:, :, :], AX.X, ALU.max))
                dve.tensor_tensor(shifted[:, :, :], logit[:, :, :], wide(top), ALU.subtract).then_inc(shift_done, 1)
                dve.wait_ge(ex_done, T + 1)
                after(dve.tensor_reduce(den[:, :], ex[:, :, :], AX.X, ALU.add))
                after(dve.reciprocal(rden[:, :], den[:, :]))
                after(dve.tensor_tensor(prob[:, :, :], ex[:, :, :], wide(rden), ALU.mult))
                after(dve.tensor_tensor(above[:, :, :, :], other, own, ALU.is_gt))
                after(dve.tensor_tensor(ties[:, :, :, :], other, own, ALU.is_equal))
                after(dve.tensor_tensor(ties[:, :, :, :], ties[:, :, :, :],
                                        lower[:, :, :].unsqueeze(1).to_broadcast([P, SUB, E, E]), ALU.mult))
                after(dve.tensor_tensor(above[:, :, :, :], above[:, :, :, :], ties[:, :, :, :], ALU.add))
                after(dve.tensor_reduce(rank[:, :, :], above[:, :, :, :], AX.X, ALU.add))
                after(dve.scalar_tensor_tensor(picked[:, :, :], rank[:, :, :], 1.5, prob[:, :, :], ALU.is_lt, ALU.mult))
                after(dve.tensor_reduce(psum2[:, :], picked[:, :, :], AX.X, ALU.add))
                after(dve.reciprocal(rpsum2[:, :], psum2[:, :]))
                after(dve.scalar_tensor_tensor(gate[:, :, :], picked[:, :, :], LORA_SCALING, wide(rpsum2), ALU.mult, ALU.mult))
                assert count[0] == LINKS
                gate_r = gate[:, :, :].rearrange("p s e -> p (s e)").unsqueeze(2).to_broadcast([P, SUB * E, RANK])
                dve.tensor_copy(gate_x[:, :, :].rearrange("p s (e r) -> p (s e) r", r=RANK), gate_r).then_inc(gated, 1)

            def gate_mid(T):
                dve.wait_ge(gate_turned, T + 1)
                dve.wait_ge(mid_copied, T + 1 + START)
                dve.tensor_tensor(gated_mid[:, :], lg_ps[:, :], mid[:, :], ALU.mult).then_inc(mid_gated, 1)

            def mid_rest(T):
                dve.wait_ge(mt_hi_done, T + 1)
                dve.tensor_tensor(mt_lo[:, :], gated_mid[:, :], mt_hi[:, :].bitcast(F32), ALU.subtract).then_inc(mt_lo_done, 1)

            def final(T, i, u, s):
                dve.wait_ge(out_done, 4 * T + s + 1 + START)
                if s == 0:
                    dve.wait_ge(biased, T + 1)
                    dve.wait_ge(y_stored[u], 16 * i + START)
                dve.tensor_tensor(y[:, u, s, :], out_ps[s % 2][:, :], xin[:, u, s, :], ALU.add).then_inc(y_done, 1)

            def tile(T, i, u, more, load):
                if more:
                    add(T + 1, i + u, 1 - u, 0)
                gates(T)
                if more:
                    add(T + 1, i + u, 1 - u, 1)
                gate_mid(T)
                mid_rest(T)
                if more:
                    add(T + 1, i + u, 1 - u, 2)
                    add(T + 1, i + u, 1 - u, 3)
                    variances(T + 1)
                final(T, i, u, 0)
                final(T, i, u, 1)
                if more:
                    normalise(T + 1, 1 - u)
                final(T, i, u, 2)
                if more:
                    for kt in range(KT):
                        xt_rest(T + 1, 1 - u, kt)
                if load:
                    ctx_rest(T + 2, u)
                final(T, i, u, 3)

            dve.sem_inc(added, AHEAD)
            dve.sem_inc(y_done, FREE)
            for n in range(KT):
                weights.rest(dve, n)
            ctx_rest(0, 0)
            for n in range(KT, len(jobs)):
                weights.rest(dve, n)
            ctx_rest(1, 1)
            dve.wait_ge(consts_done, 2)
            dve.wait_ge(bias_loaded, 32)
            for s in range(SUB):
                add(0, 0, 0, s)
            variances(0)
            normalise(0, 0)
            for kt in range(KT):
                xt_rest(0, 0, kt)
            with dve.Fori(0, TILES // 2 - 1) as i:
                for u in range(2):
                    tile(2 * i + u, i, u, True, True)
            tile(TILES - 2, TILES // 2 - 1, 0, True, False)
            tile(TILES - 1, TILES // 2 - 1, 1, False, False)


def layer(nc, x, wq_t, wk_t, wv_t, wo_t, rope, base_t, base_b, router_t, router_b, lora_a, lora_b, out):
    qk_scr = nc.dram_tensor("qk_scratch", [4, GROUPS, P, SEQ], F32, kind="Internal").ap()
    v_scr = nc.dram_tensor("v_scratch", [GROUPS, SEQ, P], F32, kind="Internal").ap()
    ctx_scr = nc.dram_tensor("ctx_scratch", [GROUPS, P, SEQ], F32, kind="Internal").ap()
    project(nc, x, wq_t, wk_t, wv_t, rope, qk_scr, v_scr)
    attend(nc, qk_scr, v_scr, ctx_scr)
    finish(nc, x, ctx_scr, wo_t, base_t, base_b, router_t, router_b, lora_a, lora_b, out)


def rope_tables():
    inv = np.exp(np.float32(-np.log(THETA)) * np.arange(0, DK, 2, dtype=np.float32) / np.float32(DK)).astype(np.float32)
    angle = (np.arange(SEQ, dtype=np.float32)[None, :] * inv[:, None]).astype(np.float32).astype(np.float64)
    one = np.stack([-np.sin(angle), np.cos(angle), np.sin(angle)], axis=1).astype(np.float32)
    return np.ascontiguousarray(np.tile(one, (P // (DK // 2), 1, BATCH)))


def kernel(L0_attn_x, L0_attn_Wq, L0_attn_Wk, L0_attn_Wv, L0_attn_Wo, L0_ffn_base_w, L0_ffn_base_b,
           L0_ffn_router_w, L0_ffn_router_b, L0_ffn_lora_A, L0_ffn_lora_B):
    import concourse.bacc as bacc
    from concourse.bass_utils import run_bass_kernel_spmd

    def turned(w):
        return np.ascontiguousarray(np.transpose(np.asarray(w)))

    def halves(w):
        return np.ascontiguousarray(np.asarray(w).reshape(2, 8, DK // 2, 2, DM).transpose(4, 0, 3, 1, 2).reshape(DM, DM))

    arrays = {
        "x": np.asarray(L0_attn_x).reshape(TOKENS, DM),
        "wq_t": halves(L0_attn_Wq),
        "wk_t": halves(L0_attn_Wk),
        "wv_t": turned(L0_attn_Wv),
        "wo_t": turned(L0_attn_Wo),
        "rope": rope_tables(),
        "base_t": turned(L0_ffn_base_w),
        "base_b": np.asarray(L0_ffn_base_b).reshape(1, DM),
        "router_t": turned(L0_ffn_router_w),
        "router_b": np.asarray(L0_ffn_router_b).reshape(1, EXPERTS),
        "lora_a": np.ascontiguousarray(np.asarray(L0_ffn_lora_A).transpose(1, 0, 2).reshape(DM, EXPERTS * RANK)),
        "lora_b": np.asarray(L0_ffn_lora_B).reshape(EXPERTS * RANK, DM),
    }
    nc = bacc.Bacc("TRN2", target_bir_lowering=False, num_devices=1)
    args = [nc.dram_tensor(f"in_{name}", a.shape, F32, kind="ExternalInput").ap() for name, a in arrays.items()]
    out = nc.dram_tensor("out", [TOKENS, DM], F32, kind="ExternalOutput").ap()
    nc.disable_value_cache = True
    layer(nc, *args, out)
    r = run_bass_kernel_spmd(nc, [{f"in_{name}": a for name, a in arrays.items()}], core_ids=[0])
    return r.results[0]["out"].reshape(BATCH, SEQ, DM)
```

```python
from contextlib import ExitStack

import numpy as np

import concourse.bass as bass
from concourse import mybir

F32 = mybir.dt.float32
F32R = mybir.dt.float32r
BF16 = mybir.dt.bfloat16
ALU = mybir.AluOpType
ACT = mybir.ActivationFunctionType
AX = mybir.AxisListType

P = 128
BATCH, SEQ, DM = 2, 2048, 512
HEADS, DK = 16, 32
EXPERTS, RANK = 8, 16
TOKENS = BATCH * SEQ
KT = DM // P
TT = 512
TILES = TOKENS // TT
SUB = TT // P
HG = 4
GROUPS = BATCH * HEADS // HG
QT = SEQ // TT
KB = SEQ // P
EPS = 1e-5
THETA = 10000.0
LORA_SCALING = 2.0
SCORE_SCALE = 1.0 / float(np.sqrt(DK))
MASKED = -1e38
W_RING = 4
START = 1

STEPS = [(t, j) for t in range(QT) for j in range((t + 1) * SUB)]
NSTEP = len(STEPS)
UNIT_END = [STEPS.index((t, (t + 1) * SUB - 1)) for t in range(QT)]
NPAIR = NSTEP // 2
LAG = 2
RING = 5
ITEMS = [(t, qi, h, c) for t in range(QT) for qi in range(SUB) for h in range(HG) for c in range(t + 1)]
NITEM = len(ITEMS)
ITEM_END = [max(n for n, it in enumerate(ITEMS) if it[0] == t) for t in range(QT)]
HEAD_START = NITEM // 2 + 5
PER_FIRST = 7
BEFORE_FIRST = ITEM_END[1] + 1


def width(s):
    t, j = STEPS[s % NSTEP]
    return 1.0 - max(0, j - t * SUB) / SUB


def plan_items():
    room = [width(s + 1) + width(s) + width(s - LAG) * ((s - LAG) % 2) + 1.0 for s in range(NSTEP)]
    for e in UNIT_END:
        room[(e + LAG) % NSTEP] -= 0.8
        room[(e + LAG + 1) % NSTEP] -= 0.5
    done = [sum(room[:s]) / sum(room) * NITEM for s in range(NSTEP + 1)]
    return [HEAD_START + round(d) for d in done]


PLAN = plan_items()


def items_before(s, first):
    steady = PLAN[s % NSTEP] + NITEM * (s // NSTEP)
    return min(BEFORE_FIRST + PER_FIRST * s, steady) if first else steady


def items_of_step(s, first):
    return [(f // NITEM, f % NITEM) for f in range(items_before(s, first), items_before(s + 1, first))]


def units_ended_at_step(s, first):
    return [(n, ITEMS[k][0]) for n, k in items_of_step(s, first) if k in ITEM_END]


def unit_ended_before(s, steps):
    e = s - steps
    return [(int(e < 0), t) for t in range(QT) if UNIT_END[t] == e % NSTEP]


def wait_alone(eng, semaphore, value, passed):
    eng.wait_ge(semaphore, value)
    eng.sem_inc(passed, 1)


def units_ended_at_step(s, first):
    return [(n, ITEMS[k][0]) for n, k in items_of_step(s, first) if k in ITEM_END]


class Weights:

    def __init__(self, jobs, raw, loaded, hi_done, lo_done):
        self.jobs, self.raw, self.loaded, self.hi_done, self.lo_done = jobs, raw, loaded, hi_done, lo_done

    def staging(self, n):
        return self.raw[:, n % len(self.loaded), 0:self.jobs[n][0].shape[-1]]

    def load(self, eng, n):
        ring = len(self.loaded)
        if n >= ring:
            eng.wait_ge(self.lo_done, n - ring + 1)
        eng.dma_start(self.staging(n), self.jobs[n][0]).then_inc(self.loaded[n % ring], 16)

    def round(self, act, n):
        ring = len(self.loaded)
        act.wait_ge(self.loaded[n % ring], 16 * (n // ring + 1))
        act.activation(self.jobs[n][1], self.staging(n), ACT.Copy).then_inc(self.hi_done, 1)

    def rest(self, dve, n):
        dve.wait_ge(self.hi_done, n + 1)
        dve.tensor_tensor(self.jobs[n][2], self.staging(n), self.jobs[n][1].bitcast(F32),
                          ALU.subtract).then_inc(self.lo_done, 1)


def project(nc, x, wq_t, wk_t, wv_t, rope, qk_scr, v_scr, shared):
    x_v = x.rearrange("(t s p) d -> t p s d", p=P, s=SUB)
    rope_v = rope.rearrange("p c (t n) -> t p c n", n=TT)
    with ExitStack() as ctx:
        def sb(name, shape, dt=F32):
            return ctx.enter_context(nc.sbuf_tensor(name, shape, dt))

        def sem(name):
            return ctx.enter_context(nc.semaphore(name))

        w_raw = shared.rearrange("p (n d) -> p n d", d=DM)
        w_hi = sb("p_w_hi", [P, KT, 3 * DM], F32R)
        w_lo = sb("p_w_lo", [P, KT, 3 * DM], F32R)
        ident = sb("p_ident", [P, P])
        xb = sb("p_x", [P, 2, SUB, DM])
        stats = sb("p_stats", [P, SUB, 6])
        mv = sb("p_mv", [P, SUB, 2])
        std = sb("p_std", [P, SUB])
        rstd = sb("p_rstd", [P, SUB])
        xt_hi = sb("p_xt_hi", [P, 2, KT, TT], F32R)
        xt_lo = sb("p_xt_lo", [P, 2, KT, TT], F32R)
        tab = sb("p_tab", [P, 2, 3, TT])
        mul = sb("p_mul", [P, 2, 2, 2, TT])
        rot = sb("p_rot", [P, 2, 2, TT])
        rot_hi = sb("p_rot_hi", [P, 2, 2, TT], F32R)
        rot_lo = sb("p_rot_lo", [P, 2, 2, TT], F32R)
        v_st = sb("p_v_st", [P, 2, SUB, DM])
        pair_ps = [ctx.enter_context(nc.psum_tensor(f"p_pair{n}", [P, 2, TT], F32)) for n in range(2)]
        tr_ps = [ctx.enter_context(nc.psum_tensor(f"p_tr{n}", [P, TT], F32)) for n in range(2)]
        v_ps = [ctx.enter_context(nc.psum_tensor(f"p_v{n}", [P, DM], F32)) for n in range(2)]

        w_loaded = [sem(f"p_w_loaded{n}") for n in range(W_RING)]
        w_hi_done, w_lo_done = sem("p_w_hi_done"), sem("p_w_lo_done")
        zeroed, ident_done = sem("p_zeroed"), sem("p_ident_done")
        x_loaded = [sem("p_x_loaded0"), sem("p_x_loaded1")]
        tab_loaded = [sem("p_tab_loaded0"), sem("p_tab_loaded1")]
        stats_done, var_done, std_done = sem("p_stats_done"), sem("p_var_done"), sem("p_std_done")
        passed = sem("p_passed")
        rstd_done, xn_done = sem("p_rstd_done"), sem("p_xn_done")
        tr_done, xt_hi_done, xt_lo_done = sem("p_tr_done"), sem("p_xt_hi_done"), sem("p_xt_lo_done")
        pair_done, v_done, v_copied = sem("p_pair_done"), sem("p_v_done"), sem("p_v_copied")
        mul_done, rot_done = sem("p_mul_done"), sem("p_rot_done")
        rot_hi_done, rot_lo_done = sem("p_rot_hi_done"), sem("p_rot_lo_done")
        rot_stored = [sem("p_rot_stored0"), sem("p_rot_stored1")]
        v_stored = [sem("p_v_stored0"), sem("p_v_stored1")]
        AHEAD = 2

        block = ctx.enter_context(nc.Block())
        jobs = [(w[kt * P:(kt + 1) * P, :], w_hi[:, kt, n * DM:(n + 1) * DM], w_lo[:, kt, n * DM:(n + 1) * DM])
                for n, w in ((0, wq_t), (2, wv_t), (1, wk_t)) for kt in range(KT)]

        weights = Weights(jobs, w_raw, w_loaded, w_hi_done, w_lo_done)

        @block.gpsimd
        def _(pool):
            for semaphore in (v_done, *rot_stored, *v_stored):
                pool.sem_inc(semaphore, START)
            pool.memset(ident[:, :], 0.0).then_inc(zeroed, 1)
            pool.wait_ge(zeroed, 1)
            pool.affine_select(ident[:, :], ident[:, :], pattern=[[-1, P]], compare_op=ALU.not_equal,
                               fill=1.0, base=0, channel_multiplier=1).then_inc(ident_done, 1)

            def rope_sum(m, par):
                pool.wait_ge(mul_done, m + 1 + AHEAD)
                pool.wait_ge(rot_lo_done, m + 1)
                pool.tensor_tensor(rot[:, par], mul[:, par, :, 0, :], mul[:, par, :, 1, :],
                                   ALU.add).then_inc(rot_done, 1)

            pool.sem_inc(rot_done, AHEAD)
            with pool.Fori(0, TILES) as T:
                for p in range(4):
                    rope_sum(4 * T + p, p % 2)

        @block.sync
        def _(sp):
            for s in range(SUB):
                sp.dma_start(xb[:, 0, s], x_v[0][:, s]).then_inc(x_loaded[0], 16)
            for n in range(2 * KT):
                weights.load(sp, n)
            sp.dma_start(tab[:, 0], rope_v[0]).then_inc(tab_loaded[0], 16)
            for n in range(2 * KT, len(jobs)):
                weights.load(sp, n)
            sp.dma_start(xb[:, 1], x_v[1]).then_inc(x_loaded[1], 16)
            sp.dma_start(tab[:, 1], rope_v[1]).then_inc(tab_loaded[1], 16)
            with sp.Fori(0, BATCH) as b:
                with sp.Fori(0, 2) as half:
                    for u in range(2):
                        T = 4 * b + 2 * half + u
                        tok = bass.ds(1024 * half + 512 * u, TT)
                        for p in range(4):
                            if p == 3:
                                sp.wait_ge(v_copied, 4 * T + 4 + AHEAD)
                                for hg in range(4):
                                    dst = v_scr[4 * b + hg][tok, :].rearrange("(s p) c -> p s c", p=P)
                                    sp.dma_start(dst, v_st[:, u, :, hg * P:(hg + 1) * P]).then_inc(v_stored[u], 16)
                            m = 4 * T + p
                            rows = bass.ds(512 * b + 256 * (p % 2), 256)
                            sp.wait_ge(rot_lo_done, m + 1 + AHEAD)
                            for n, src in enumerate((rot_hi, rot_lo)):
                                dst = qk_scr[2 * (p // 2) + n].rearrange("g r n -> (g r) n")[rows, tok]
                                sp.dma_start(dst.rearrange("(p a) n -> p a n", a=2),
                                             src[:, p % 2].bitcast(F32)).then_inc(rot_stored[p % 2], 16)
            for u in range(2):
                sp.wait_ge(rot_stored[u], 32 * 2 * TILES + START)
                sp.wait_ge(v_stored[u], 64 * TILES // 2 + START)

        @block.tensor
        def _(pe):
            pe.wait_ge(ident_done, 1)

            def transposes(T, u, features):
                pe.wait_ge(xn_done, T + 1)
                for kt in features:
                    if isinstance(T, int) and 4 * T + kt - 1 <= 0:
                        pass
                    else:
                        pe.wait_ge(xt_lo_done, 4 * T + kt - 1)
                    for s in range(SUB):
                        mm = pe.transpose(tr_ps[kt % 2][:, s * P:(s + 1) * P],
                                          xb[:, u, s, kt * P:(kt + 1) * P], ident[:, :])
                    mm.then_inc(tr_done, 1)

            def qk_pair(T, u, p):
                pe.wait_ge(mul_done, 4 * T + p + 1)
                pe.wait_ge(w_lo_done, KT if p < 2 else 3 * KT)
                for half in range(2):
                    cols = slice((2 * p + half) * P, (2 * p + half + 1) * P)
                    passes = [(w, a, kt) for w, a in ((w_hi, xt_hi), (w_lo, xt_hi), (w_hi, xt_lo)) for kt in range(KT)]
                    for n, (w, a, kt) in enumerate(passes):
                        mm = pe.matmul(pair_ps[p % 2][:, half, :], w[:, kt, cols], a[:, u, kt, :],
                                       start=(n == 0), stop=(n == len(passes) - 1))
                mm.then_inc(pair_done, 1)

            def v_sub(T, u, s):
                pe.wait_ge(v_copied, 4 * T + s + 1)
                pe.wait_ge(w_lo_done, 2 * KT)
                passes = [(a, w, kt) for a, w in ((xt_hi, w_hi), (xt_hi, w_lo), (xt_lo, w_hi)) for kt in range(KT)]
                for n, (a, w, kt) in enumerate(passes):
                    mm = pe.matmul(v_ps[s % 2][:, :], a[:, u, kt, s * P:(s + 1) * P], w[:, kt, 2 * DM:3 * DM],
                                   start=(n == 0), stop=(n == len(passes) - 1))
                mm.then_inc(v_done, 1)

            def tile(T, u, more):
                pe.wait_ge(xt_lo_done, 4 * T + 4)
                for p in range(4):
                    qk_pair(T, u, p)
                    v_sub(T, u, p)
                    if p == 1 and more:
                        transposes(T + 1, 1 - u, (0, 1))
                    if p == 2 and more:
                        transposes(T + 1, 1 - u, (2, 3))

            transposes(0, 0, range(KT))
            with pe.Fori(0, TILES // 2 - 1) as i:
                for u in range(2):
                    tile(2 * i + u, u, True)
            tile(TILES - 2, 0, True)
            tile(TILES - 1, 1, False)

        @block.scalar
        def _(act):
            def load_x(T, u):
                act.dma_start(xb[:, u], x_v[T]).then_inc(x_loaded[u], 16)

            def load_tab(T, u):
                act.dma_start(tab[:, u], rope_v[T]).then_inc(tab_loaded[u], 16)

            def root(T):
                act.wait_ge(var_done, T + 1)
                act.activation(std[:, :], mv[:, :, 1], ACT.Sqrt, bias=EPS).then_inc(std_done, 1)

            def xt_copy(T, u, kt):
                act.wait_ge(tr_done, 4 * T + kt + 1)
                act.activation(xt_hi[:, u, kt, :], tr_ps[kt % 2][:, :], ACT.Copy).then_inc(xt_hi_done, 1)

            def rot_copy(T, i, p):
                act.wait_ge(rot_done, 4 * T + p + 1 + AHEAD)
                act.wait_ge(rot_stored[p % 2], 32 * (2 * T + p // 2) + START)
                act.activation(rot_hi[:, p % 2], rot[:, p % 2], ACT.Copy).then_inc(rot_hi_done, 1)

            def v_copy(T, i, u, s):
                act.wait_ge(v_done, 4 * T + s + 1 + START)
                if s == 0:
                    act.wait_ge(v_stored[u], 64 * i + START)
                act.activation(v_st[:, u, s, :], v_ps[s % 2][:, :], ACT.Copy).then_inc(v_copied, 1)

            def tile(T, i, u, more, load):
                if load:
                    load_x(T + 2, u)
                if more:
                    root(T + 1)
                v_copy(T, i, u, 0)
                rot_copy(T, i, 0)
                v_copy(T, i, u, 1)
                if more:
                    act.wait_ge(v_done, 4 * T + START)
                    for kt in (0, 1):
                        xt_copy(T + 1, 1 - u, kt)
                rot_copy(T, i, 1)
                v_copy(T, i, u, 2)
                if more:
                    for kt in (2, 3):
                        xt_copy(T + 1, 1 - u, kt)
                rot_copy(T, i, 2)
                v_copy(T, i, u, 3)
                rot_copy(T, i, 3)
                if load:
                    act.wait_ge(mul_done, 4 * T + 4 + AHEAD)
                    load_tab(T + 2, u)

            for n in range(KT):
                weights.round(act, n)
            root(0)
            for kt in range(KT):
                xt_copy(0, 0, kt)
            for n in range(KT, len(jobs)):
                weights.round(act, n)
            act.sem_inc(v_copied, AHEAD)
            with act.Fori(0, TILES // 2 - 1) as i:
                for u in range(2):
                    tile(2 * i + u, i, u, True, True)
            tile(TILES - 2, TILES // 2 - 1, 0, True, False)
            tile(TILES - 1, TILES // 2 - 1, 1, False, False)

        @block.vector
        def _(dve):
            def layer_norm(T, i, u):
                if isinstance(T, int) and T == 0:
                    dve.wait_ge(x_loaded[0], 16 * SUB)
                else:
                    dve.wait_ge(x_loaded[u], 16 * i + (16 * SUB if u == 0 else 16))
                if not (isinstance(T, int) and T == 0):
                    dve.wait_ge(xn_done, T)
                for s in range(SUB):
                    ins = dve.bn_stats(stats[:, s, :], xb[:, u, s, :])
                ins.then_inc(stats_done, 1)
                wait_alone(dve, stats_done, T + 1, passed)
                for s in range(SUB):
                    ins = dve.bn_aggr(mv[:, s, :], stats[:, s, :])
                ins.then_inc(var_done, 1)
                dve.wait_ge(std_done, T + 1)
                dve.reciprocal(rstd[:, :], std[:, :]).then_inc(rstd_done, 1)
                dve.wait_ge(rstd_done, T + 1)
                for s in range(SUB):
                    ins = dve.tensor_scalar(xb[:, u, s, :], xb[:, u, s, :], mv[:, s, 0:1], rstd[:, s:s + 1],
                                            ALU.subtract, ALU.mult)
                ins.then_inc(xn_done, 1)

            def xt_rest(T, u, kt):
                dve.wait_ge(xt_hi_done, 4 * T + kt + 1)
                dve.tensor_tensor(xt_lo[:, u, kt, :], tr_ps[kt % 2][:, :], xt_hi[:, u, kt, :].bitcast(F32),
                                  ALU.subtract).then_inc(xt_lo_done, 1)

            def rope_mul(T, i, u, p):
                if p == 0:
                    dve.wait_ge(tab_loaded[u], 16 * i + 16)
                dve.wait_ge(pair_done, 4 * T + p + 1)
                dve.wait_ge(rot_done, 4 * T + p + 1)
                even, odd = (pair_ps[p % 2][:, n:n + 1, :].to_broadcast([P, 2, TT]) for n in range(2))
                dve.tensor_tensor(mul[:, p % 2, :, 0, :], even, tab[:, u, 1:3, :], ALU.mult)
                dve.tensor_tensor(mul[:, p % 2, :, 1, :], odd, tab[:, u, 0:2, :], ALU.mult).then_inc(mul_done, 1)

            def rot_rest(T, p):
                dve.wait_ge(rot_hi_done, 4 * T + p + 1)
                dve.tensor_tensor(rot_lo[:, p % 2], rot[:, p % 2], rot_hi[:, p % 2].bitcast(F32),
                                  ALU.subtract).then_inc(rot_lo_done, 1)

            def tile(T, i, u, more):
                if more:
                    layer_norm(T + 1, i + u, 1 - u)
                rope_mul(T, i, u, 0)
                rope_mul(T, i, u, 1)
                rot_rest(T, 0)
                if more:
                    for kt in (0, 1):
                        xt_rest(T + 1, 1 - u, kt)
                rope_mul(T, i, u, 2)
                rot_rest(T, 1)
                if more:
                    for kt in (2, 3):
                        xt_rest(T + 1, 1 - u, kt)
                rope_mul(T, i, u, 3)
                rot_rest(T, 2)
                rot_rest(T, 3)

            dve.sem_inc(mul_done, AHEAD)
            dve.sem_inc(rot_lo_done, AHEAD)
            layer_norm(0, 0, 0)
            for n in range(KT):
                weights.rest(dve, n)
            for kt in range(KT):
                xt_rest(0, 0, kt)
            for n in range(KT, len(jobs)):
                weights.rest(dve, n)
            with dve.Fori(0, TILES // 2 - 1) as i:
                for u in range(2):
                    tile(2 * i + u, i, u, True)
            tile(TILES - 2, TILES // 2 - 1, 0, True)
            tile(TILES - 1, TILES // 2 - 1, 1, False)


def attend(nc, qk_scr, v_scr, ctx_scr, shared, early):
    with ExitStack() as ctx:
        def sb(name, shape, dt=F32):
            return ctx.enter_context(nc.sbuf_tensor(name, shape, dt))

        def sem(name):
            return ctx.enter_context(nc.semaphore(name))

        BANKS = 3
        q_stack = sb("a_q_stack", [P, QT, HG, TT], F32R)
        k_stack = [sb(f"a_k_stack{n}", [P, HG, SEQ], F32R) for n in range(2)]
        vb = [shared.rearrange("p (j c) -> p j c", c=P), sb("a_v1", [P, KB, P])]
        probs = sb("a_probs", [P, RING, HG, TT])
        pair = sb("a_pair", [P, 2, HG, TT])
        ctx_st = sb("a_ctx_st", [P, 2, TT])
        sum_t = sb("a_sum_t", [P, TT])
        rsum = sb("a_rsum", [P, TT // 32])
        rsum_b = sb("a_rsum_b", [P, TT])
        mask = sb("a_mask", [P, TT])
        ones = sb("a_ones", [P, DK])
        eye = sb("a_eye", [P, P], BF16)
        later = sb("a_later", [P, P], BF16)
        part = sb("a_part", [P, HG * SUB, QT])
        neg_max = sb("a_neg_max", [P, HG * SUB])
        neg_parts = sb("a_neg_parts", [P, 2, HG, SUB])
        neg_rows = sb("a_neg_rows", [P, 2, 32])
        st_ps = ctx.enter_context(nc.psum_tensor("a_st", [P, BANKS, TT], F32))
        mx_ps = [ctx.enter_context(nc.psum_tensor(f"a_mx{n}", [P, TT], F32)) for n in range(BANKS)]
        av_ps = ctx.enter_context(nc.psum_tensor("a_av", [P, TT], F32))
        sum_ps = ctx.enter_context(nc.psum_tensor("a_sum", [P, TT], F32))

        kv_loaded = [sem("a_kv_loaded0"), sem("a_kv_loaded1")]
        first_keys = [sem(f"a_first_keys{c}") for c in range(QT)]
        first_values = sem("a_first_values")
        q_loaded = [sem(f"a_q_loaded{t}") for t in range(QT)]
        shift_loaded = [sem("a_shift_loaded0"), sem("a_shift_loaded1")]
        consts_done, zeroed = sem("a_consts_done"), sem("a_zeroed")
        mask_done, key_ones, ones_done = sem("a_mask_done"), sem("a_key_ones"), sem("a_ones_done")
        st_done, exp_done, step_done = sem("a_st_done"), sem("a_exp_done"), sem("a_step_done")
        pair_added, pair_done = sem("a_pair_added"), sem("a_pair_done")
        av_copied, sum_turned = sem("a_av_copied"), sem("a_sum_turned")
        item_done, max_done = sem("a_item_done"), sem("a_max_done")
        dve_passed, reduced, rounded = sem("a_dve_passed"), sem("a_reduced"), sem("a_rounded")
        rsum_done, rsum_turned, out_done = sem("a_rsum_done"), sem("a_rsum_turned"), sem("a_out_done")
        neg_done, rows_done = sem("a_neg_done"), sem("a_rows_done")
        ctx_stored = [sem("a_ctx_stored0"), sem("a_ctx_stored1")]
        KV_LOADS, Q_LOADS, SHIFTS = 16 * 5, 16 * 3, 16 * 4
        FREE = (RING + 1) // 2

        block = ctx.enter_context(nc.Block())

        def exps(g, s, h):
            return HG * NSTEP * g + HG * s + h + 1 + BANKS

        def prior_use(n, of):
            return n - BANKS if n >= BANKS else max(m for m in range(of) if m % BANKS == n) - of

        def pairs(g, p):
            return NPAIR * g + p + 1 + FREE

        @block.sync
        def _(sp):
            def load_kv(g, par):
                for n, kind in enumerate((2, 3, 2)):
                    sp.dma_start(k_stack[par][32 * n:32 * n + 32].bitcast(F32),
                                 qk_scr[kind, g].rearrange("(h r) n -> r h n", r=DK)).then_inc(kv_loaded[par], 16)
                v_rows = v_scr[g].rearrange("(a j p) c -> a p j c", p=P, a=2)
                for n in range(2):
                    sp.dma_start(vb[par][:, n * KB // 2:(n + 1) * KB // 2], v_rows[n]).then_inc(kv_loaded[par], 16)

            def load_first_keys(c):
                for n, kind in enumerate((2, 3, 2)):
                    sp.dma_start(k_stack[0][32 * n:32 * n + 32, :, c * TT:(c + 1) * TT].bitcast(F32),
                                 qk_scr[kind, 0].rearrange("(h r) n -> r h n", r=DK)[:, :, c * TT:(c + 1) * TT]
                                 ).then_inc(first_keys[c], 16)

            def load_q(g, t):
                for n, kind in enumerate((0, 0, 1)):
                    sp.dma_start(q_stack[32 * n:32 * n + 32, t].bitcast(F32),
                                 qk_scr[kind, g].rearrange("(h r) n -> r h n", r=DK)[:, :, t * TT:(t + 1) * TT]
                                 ).then_inc(q_loaded[t], 16)

            def shift_rows(g, t):
                sp.wait_ge(rows_done, 4 * g + t + 1 + START)
                dst = q_stack[96:98, t].bitcast(F32).rearrange("p h (q c r) -> p (h q) c r", c=4, r=32)
                for quarter in range(4):
                    sp.dma_start(dst[:, :, quarter], neg_rows[32 * quarter:32 * quarter + 32, t % 2, :]
                                 ).then_inc(shift_loaded[t % 2], 16)

            def store(g, t):
                sp.wait_ge(out_done, 4 * g + t + 1 + START)
                sp.dma_start(ctx_scr[g][:, t * TT:(t + 1) * TT], ctx_st[:, t % 2]).then_inc(ctx_stored[t % 2], 16)

            def group(g, par, first, last):
                if not last:
                    if not first:
                        sp.wait_ge(step_done, NSTEP * g)
                    load_kv(g + 1, 1 - par)
                for s in range(NSTEP):
                    for nxt, t in units_ended_at_step(s, first):
                        if not (nxt and last):
                            shift_rows(g + nxt, t)
                    if s in UNIT_END and not last:
                        sp.wait_ge(st_done, HG * (NSTEP * g + s + 1))
                        load_q(g + 1, STEPS[s][0])
                    for before, t in unit_ended_before(s, LAG + 1):
                        if not (before and first):
                            store(g - before, t)

            for t in range(QT):
                load_first_keys(t)
                load_q(0, t)
                if t == 1:
                    v_rows = v_scr[0].rearrange("(a j p) c -> a p j c", p=P, a=2)
                    for n in range(2):
                        sp.dma_start(vb[0][:, n * KB // 2:(n + 1) * KB // 2], v_rows[n]).then_inc(first_values, 16)
            for t in range(QT):
                if ITEM_END[t] < BEFORE_FIRST:
                    shift_rows(0, t)
            group(0, 0, True, False)
            with sp.Fori(0, GROUPS // 2 - 1) as i:
                group(2 * i + 1, 1, False, False)
                group(2 * i + 2, 0, False, False)
            sp.wait_ge(step_done, NSTEP * (GROUPS - 1))
            sp.wait_ge(ctx_stored[0], 16 * QT // 2 * (GROUPS - 1) + START)
            for dst, src, semaphore in early:
                sp.dma_start(dst, src).then_inc(semaphore, 16)
            group(GROUPS - 1, 1, False, True)
            store(GROUPS - 1, QT - 1)
            for n in range(2):
                sp.wait_ge(ctx_stored[n], 16 * GROUPS * QT // 2 + START)

        @block.gpsimd
        def _(pool):
            for semaphore in (av_copied, sum_turned, out_done, rows_done, *shift_loaded, *ctx_stored):
                pool.sem_inc(semaphore, START)
            for n, buffer in enumerate((mask, eye, later)):
                pool.memset(buffer[:, :], 0.0).then_inc(zeroed, 1)
                pool.wait_ge(zeroed, n + 1)
            pool.affine_select(mask[:, TT - P:TT], mask[:, TT - P:TT], pattern=[[-1, P]], compare_op=ALU.is_ge,
                               fill=MASKED, base=0, channel_multiplier=1).then_inc(mask_done, 1)
            pool.affine_select(eye[:, :], eye[:, :], pattern=[[-1, P]], compare_op=ALU.not_equal,
                               fill=1.0, base=0, channel_multiplier=1).then_inc(consts_done, 1)
            pool.affine_select(later[:, :], later[:, :], pattern=[[1, P]], compare_op=ALU.is_ge,
                               fill=MASKED, base=0, channel_multiplier=-1).then_inc(consts_done, 1)
            pool.wait_ge(consts_done, 2)
            for n in range(2):
                pool.memset(k_stack[n][96:98].bitcast(F32), 1.0).then_inc(key_ones, 1)
                pool.wait_ge(key_ones, n + 1)

            def add_pairs(g, first):
                for p in range(NPAIR):
                    s = 2 * p
                    t, j = STEPS[s]
                    q0 = max(0, j + 1 - t * SUB) * P
                    pool.wait_ge(pair_done, pairs(g, p - 2))
                    for h in range(0, HG, 2):
                        pool.wait_ge(exp_done, exps(g, s + 1, h + 1))
                        pool.tensor_tensor(pair[:, p % 2, h:h + 2, q0:TT], probs[:, s % RING, h:h + 2, q0:TT],
                                           probs[:, (s + 1) % RING, h:h + 2, q0:TT], ALU.add).then_inc(pair_added, 1)
                    for ahead, t_out in unit_ended_before(s, 1):
                        if not (ahead and first):
                            divide(g - ahead, t_out)

            def divide(g, t):
                pool.wait_ge(rsum_turned, 4 * g + t + 1)
                pool.wait_ge(av_copied, 4 * g + t + 1 + START)
                pool.tensor_tensor(ctx_st[:, t % 2], ctx_st[:, t % 2], rsum_b[:, :], ALU.mult).then_inc(out_done, 1)

            add_pairs(0, True)
            with pool.Fori(1, GROUPS) as g:
                add_pairs(g, False)
            divide(GROUPS - 1, QT - 1)

        @block.tensor
        def _(pe):
            def item(g, par, use, k):
                t, qi, h, c = ITEMS[k]
                width = TT if c < t else (qi + 1) * P
                if k == 0 and use is not None:
                    pe.wait_ge(kv_loaded[par], KV_LOADS * use + KV_LOADS)
                if k == 0 or k - 1 in ITEM_END:
                    if use is None:
                        pe.wait_ge(first_keys[t], 3 * 16)
                    pe.wait_ge(q_loaded[t], Q_LOADS * g + Q_LOADS)
                pe.wait_ge(max_done, NITEM * g + prior_use(k, NITEM) + 1 + BANKS)
                pe.matmul(mx_ps[k % BANKS][:, 0:width], q_stack[0:96, t, h, qi * P:(qi + 1) * P],
                          k_stack[par][0:96, h, c * TT:c * TT + width], start=True, stop=True).then_inc(item_done, 1)

            def scores(g, par, s, h):
                t, j = STEPS[s]
                diagonal = j >= t * SUB
                q0 = max(0, j - t * SUB) * P
                if j == 0 and h == 0:
                    pe.wait_ge(shift_loaded[t % 2], SHIFTS * (2 * g + t // 2 + 1) + START)
                n = HG * s + h
                pe.wait_ge(exp_done, HG * NSTEP * g + prior_use(n, HG * NSTEP) + 1 + BANKS)
                mm = pe.matmul(st_ps[:, n % BANKS, q0:TT], k_stack[par][0:98, h, j * P:(j + 1) * P],
                               q_stack[0:98, t, h, q0:TT], start=True, stop=not diagonal)
                if diagonal:
                    mm = pe.matmul(st_ps[:, n % BANKS, q0:q0 + P], eye[:, :], later[:, :], start=False, stop=True)
                mm.then_inc(st_done, 1)

            def values(g, par, s):
                t, j = STEPS[s]
                q0 = max(0, j - t * SUB) * P
                if j == 0:
                    pe.wait_ge(av_copied, 4 * g + t + START)
                for h in range(HG):
                    pe.wait_ge(exp_done, exps(g, s, h))
                    mm = pe.matmul(av_ps[h * DK:(h + 1) * DK, q0:TT], vb[par][:, j, h * DK:(h + 1) * DK],
                                   probs[:, s % RING, h, q0:TT], start=(j == 0), stop=s in UNIT_END,
                                   tile_position=(0, h * DK))
                mm.then_inc(step_done, 1)

            def sums(g, p):
                s = 2 * p
                t, j = STEPS[s]
                first, last = j == 0, s + 1 in UNIT_END
                q0 = max(0, j - t * SUB) * P
                q1 = max(0, j + 1 - t * SUB) * P
                if first:
                    pe.wait_ge(sum_turned, 4 * g + t + START)
                for h in range(HG):
                    rows = slice(h * DK, (h + 1) * DK)
                    if q1 > q0:
                        pe.matmul(sum_ps[rows, q0:q1], ones[:, :], probs[:, s % RING, h, q0:q1],
                                  start=first, stop=False, tile_position=(0, h * DK))
                for h in range(HG):
                    rows = slice(h * DK, (h + 1) * DK)
                    if h % 2 == 0:
                        pe.wait_ge(pair_added, 2 * (NPAIR * g + p) + h // 2 + 1)
                    mm = pe.matmul(sum_ps[rows, q1:TT], ones[:, :], pair[:, p % 2, h, q1:TT],
                                   start=first and q1 == q0, stop=last, tile_position=(0, h * DK))
                mm.then_inc(pair_done, 1)

            def group(g, par, use, next_use, first, last):
                for s in range(NSTEP):
                    items = [(n, k) for n, k in items_of_step(s, first) if not (n and last)]
                    issued = 0
                    add_pair = (s - LAG) % 2 == 1 and not (s < LAG and first)
                    total = width(s + 1) + width(s) + (width(s - LAG) if add_pair else 0.0)

                    def items_due(work):
                        nonlocal issued
                        while issued < len(items) and issued * total <= work * len(items) + 1e-6:
                            n, k = items[issued]
                            item(g + n, (par + n) % 2, next_use if n else use, k)
                            issued += 1

                    def next_scores(h):
                        items_due(work)
                        if s + 1 < NSTEP:
                            scores(g, par, s + 1, h)
                        elif not last:
                            scores(g + 1, 1 - par, 0, h)
                        return width(s + 1) / HG

                    work = 0.0
                    work += next_scores(0)
                    work += next_scores(1)
                    items_due(work)
                    if add_pair:
                        if s < LAG:
                            sums(g - 1, (s - LAG + NSTEP) // 2)
                        else:
                            sums(g, (s - LAG) // 2)
                        work += width(s - LAG)
                    work += next_scores(2)
                    items_due(work)
                    values(g, par, s)
                    work += width(s)
                    work += next_scores(3)
                    items_due(total)

            pe.wait_ge(mask_done, 1)
            for k in range(BEFORE_FIRST):
                item(0, 0, None, k)
            pe.wait_ge(consts_done, 2)
            pe.wait_ge(key_ones, 2)
            pe.wait_ge(ones_done, 1)
            for h in range(HG):
                scores(0, 0, 0, h)
            pe.wait_ge(first_values, 2 * 16)
            group(0, 0, None, 0, True, False)
            with pe.Fori(0, GROUPS // 2 - 1) as i:
                group(2 * i + 1, 1, i, i, False, False)
                group(2 * i + 2, 0, i, i + 1, False, False)
            group(GROUPS - 1, 1, GROUPS // 2 - 1, None, False, True)
            sums(GROUPS - 1, NPAIR - 1)

        @block.scalar
        def _(act):
            def copy_values(g, t):
                act.wait_ge(step_done, NSTEP * g + UNIT_END[t] + 1)
                act.wait_ge(ctx_stored[t % 2], 16 * (2 * g + t // 2) + START)
                act.activation(ctx_st[:, t % 2], av_ps[:, :], ACT.Copy).then_inc(av_copied, 1)

            def group(g, first):
                for s, (t, j) in enumerate(STEPS):
                    q0 = max(0, j - t * SUB) * P
                    act.wait_ge(pair_done, pairs(g, (s - RING) // 2))
                    for h in range(HG):
                        act.wait_ge(st_done, HG * NSTEP * g + HG * s + h + 1)
                        act.activation(probs[:, s % RING, h, q0:TT], st_ps[:, (HG * s + h) % BANKS, q0:TT], ACT.Exp,
                                       scale=SCORE_SCALE).then_inc(exp_done, 1)
                    for before, t_out in unit_ended_before(s, 1):
                        if not (before and first):
                            copy_values(g - before, t_out)

            act.sem_inc(exp_done, BANKS)
            group(0, True)
            with act.Fori(1, GROUPS) as g:
                group(g, False)
            copy_values(GROUPS - 1, QT - 1)

        @block.vector
        def _(dve):
            def item_max(g, k):
                t, qi, h, c = ITEMS[k]
                out = part[:, h * SUB + qi, c:c + 1]
                if c < t:
                    dve.wait_ge(item_done, NITEM * g + k + 1)
                    dve.tensor_reduce(out, mx_ps[k % BANKS][:, :], AX.X, ALU.max).then_inc(max_done, 1)
                else:
                    width = (qi + 1) * P
                    wait_alone(dve, item_done, NITEM * g + k + 1, dve_passed)
                    dve.tensor_tensor_reduce(out=mx_ps[k % BANKS][:, 0:width], in0=mx_ps[k % BANKS][:, 0:width],
                                             in1=mask[:, TT - width:TT], scale=1.0, scalar=3.0 * MASKED,
                                             op0=ALU.add, op1=ALU.max, accum_out=out).then_inc(max_done, 1)

            def unit_max(g, t, items):
                U = 4 * g + t
                dve.wait_ge(max_done, items + BANKS)
                dve.tensor_reduce(neg_max[:, :], part[:, :, 0:t + 1], AX.X, ALU.max, negate=True).then_inc(reduced, 1)
                dve.wait_ge(reduced, U + 1)
                dve.wait_ge(rows_done, U + START)
                neg = neg_max[:, :].rearrange("p (h q) -> p h q", q=SUB)
                dve.tensor_copy(neg_parts[:, 0].bitcast(F32R), neg).then_inc(rounded, 1)
                dve.wait_ge(rounded, U + 1)
                dve.tensor_tensor(neg_parts[:, 1].bitcast(F32R), neg, neg_parts[:, 0], ALU.subtract).then_inc(neg_done, 1)
                dve.wait_ge(neg_done, U + 1)
                dve.wait_ge(shift_loaded[t % 2], SHIFTS * (2 * g + t // 2) + START)
                dve.transpose(neg_rows[:, t % 2, :], neg_parts[:, :, :, :].rearrange("p n h q -> p (n h q)")).then_inc(rows_done, 1)

            def turn_sums(g, t):
                dve.wait_ge(pair_done, pairs(g, UNIT_END[t] // 2))
                dve.transpose(sum_t[:, :], sum_ps[:, :]).then_inc(sum_turned, 1)

            def invert(g, t):
                dve.wait_ge(sum_turned, 4 * g + t + 1 + START)
                dve.reciprocal(rsum[:, :], sum_t[:, :].rearrange("p (b i) -> p b i", i=32)[:, :, 0]).then_inc(rsum_done, 1)

            def turn_back(g, t):
                dve.wait_ge(rsum_done, 4 * g + t + 1)
                dve.wait_ge(out_done, 4 * g + t + START)
                dve.transpose(rsum_b[:, :], rsum[:, :].unsqueeze(2).to_broadcast([P, TT // 32, 32])).then_inc(rsum_turned, 1)

            PARTS = ((turn_sums, LAG, 1.0), (invert, LAG + 1, 0.0), (turn_back, LAG + 1, 1.0))

            def group(g, first, last):
                for s in range(NSTEP):
                    items = items_of_step(s, first)
                    for n in range(max(1, len(items))):
                        if items and not (items[n][0] and last):
                            item_max(g + items[n][0], items[n][1])
                        for part_of, steps, place in PARTS:
                            for before, t in unit_ended_before(s, steps):
                                if n == round(place * max(0, len(items) - 1)) and not (before and first):
                                    part_of(g - before, t)
                    for n, t in units_ended_at_step(s, first):
                        if not (n and last):
                            issued = items_before(s + 1, first)
                            unit_max(g + n, t, NITEM * g + (min(issued, NITEM) if last else issued))

            dve.memset(ones[:, :], 1.0).then_inc(ones_done, 1)
            dve.sem_inc(max_done, BANKS)
            dve.sem_inc(pair_done, FREE)
            dve.wait_ge(mask_done, 1)
            for k in range(BEFORE_FIRST):
                item_max(0, k)
                for t in range(QT):
                    if k == ITEM_END[t]:
                        unit_max(0, t, k + 1)
            group(0, True, False)
            with dve.Fori(1, GROUPS - 1) as g:
                group(g, False, False)
            group(GROUPS - 1, False, True)
            for part_of, _, _ in PARTS:
                part_of(GROUPS - 1, QT - 1)


class Early:

    def __init__(self, nc, ctx, shared, ctx_scr, wo_t):
        self.ctx_v = ctx_scr.rearrange("(b k) p n -> b p k n", k=KT)
        self.cin = ctx.enter_context(nc.sbuf_tensor("f_ctx", [P, KT, TT], F32))[:, :, :]
        self.w_raw = shared.rearrange("p (n d) -> p n d", d=DM)
        self.ctx_loaded = ctx.enter_context(nc.semaphore("f_ctx_loaded"))
        self.w_loaded = [ctx.enter_context(nc.semaphore(f"f_w_loaded{n}")) for n in range(W_RING)]
        self.loads = [(self.w_raw[:, kt, :], wo_t[kt * P:(kt + 1) * P, :], self.w_loaded[kt]) for kt in range(KT)]
        self.loads += [(self.cin, self.ctx_v[0, :, :, 0:TT], self.ctx_loaded)]


def finish(nc, early, x, wo_t, base_t, base_b, router_t, router_b, lora_a, lora_b, out):
    ctx_v, cin, w_raw = early.ctx_v, early.cin, early.w_raw
    ctx_loaded, w_loaded = early.ctx_loaded, early.w_loaded
    x_v = x.rearrange("(t s p) d -> t p s d", p=P, s=SUB)
    out_v = out.rearrange("(t s p) d -> t p s d", p=P, s=SUB)
    E = EXPERTS
    with ExitStack() as ctx:
        def sb(name, shape, dt=F32):
            return ctx.enter_context(nc.sbuf_tensor(name, shape, dt))

        def sem(name):
            return ctx.enter_context(nc.semaphore(name))

        def psum(name, shape):
            return ctx.enter_context(nc.psum_tensor(name, shape, F32))

        wo_hi, wo_lo = sb("f_wo_hi", [P, KT, DM], F32R), sb("f_wo_lo", [P, KT, DM], F32R)
        base_hi, base_lo = sb("f_base_hi", [P, KT, DM], F32R), sb("f_base_lo", [P, KT, DM], F32R)
        a_hi, a_lo = sb("f_a_hi", [P, KT, P], F32R), sb("f_a_lo", [P, KT, P], F32R)
        r_hi, r_lo = sb("f_r_hi", [P, KT, E], F32R), sb("f_r_lo", [P, KT, E], F32R)
        b_hi, b_lo = sb("f_b_hi", [P, DM], F32R), sb("f_b_lo", [P, DM], F32R)
        bias = sb("f_bias", [P, DM])
        r_bias = sb("f_r_bias", [P, E])
        ident = sb("f_ident", [P, P])
        lower = sb("f_lower", [P, E, E])
        c_hi, c_lo = sb("f_c_hi", [P, 2, KT, TT], F32R), sb("f_c_lo", [P, 2, KT, TT], F32R)
        xin = [sb(f"f_x{n}", [P, SUB, DM]) for n in range(2)]
        xn = sb("f_xn", [P, SUB, DM])
        xt_hi, xt_lo = sb("f_xt_hi", [P, 2, KT, TT], F32R), sb("f_xt_lo", [P, 2, KT, TT], F32R)
        stats, mv = sb("f_stats", [P, SUB, 6]), sb("f_mv", [P, SUB, 2])
        std, rstd = sb("f_std", [P, SUB]), sb("f_rstd", [P, SUB])
        logit, shifted, ex, prob = (sb(f"f_g{n}", [P, SUB, E]) for n in range(4))
        rank, picked, gate = (sb(f"f_h{n}", [P, SUB, E]) for n in range(3))
        top, den, rden, psum2, rpsum2 = (sb(f"f_s{n}", [P, SUB]) for n in range(5))
        above, ties = sb("f_above", [P, SUB, E, E]), sb("f_ties", [P, SUB, E, E])
        gate_x = sb("f_gate_x", [P, SUB, P])
        logit_t = sb("f_logit_t", [E, TT])
        mid = sb("f_mid", [P, TT])
        gated_mid = sb("f_gated_mid", [P, TT])
        mt_hi, mt_lo = sb("f_mt_hi", [P, TT], F32R), sb("f_mt_lo", [P, TT], F32R)
        y = sb("f_y", [P, 2, SUB, DM])
        wo_ps = [psum(f"f_wo_ps{n}", [P, DM]) for n in range(2)]
        tr_ps = [psum(f"f_tr_ps{n}", [P, TT]) for n in range(2)]
        out_ps = [psum(f"f_out_ps{n}", [P, DM]) for n in range(2)]
        mid_ps = psum("f_mid_ps", [P, TT])
        lg_ps = psum("f_lg_ps", [P, DM])

        w_hi_done, w_lo_done = sem("f_w_hi_done"), sem("f_w_lo_done")
        x_loaded = [sem("f_x_loaded0"), sem("f_x_loaded1")]
        zeroed, consts_done, bias_loaded = sem("f_zeroed"), sem("f_consts_done"), sem("f_bias_loaded")
        c_hi_done, c_lo_done = sem("f_c_hi_done"), sem("f_c_lo_done")
        wo_done, added, stats_done, var_done = sem("f_wo_done"), sem("f_added"), sem("f_stats_done"), sem("f_var_done")
        std_done, rstd_done, xn_done, biased = sem("f_std_done"), sem("f_rstd_done"), sem("f_xn_done"), sem("f_biased")
        tr_done, xt_hi_done, xt_lo_done = sem("f_tr_done"), sem("f_xt_hi_done"), sem("f_xt_lo_done")
        router_done, mid_done, gated = sem("f_router_done"), sem("f_mid_done"), sem("f_gated")
        passed, pe_passed = sem("f_passed"), sem("f_pe_passed")
        logit_copied, logit_turned, mid_copied = sem("f_logit_copied"), sem("f_logit_turned"), sem("f_mid_copied")
        link, shift_done, ex_done = sem("f_link"), sem("f_shift_done"), sem("f_ex_done")
        gate_turned, mid_gated = sem("f_gate_turned"), sem("f_mid_gated")
        mt_hi_done, mt_lo_done = sem("f_mt_hi_done"), sem("f_mt_lo_done")
        out_done, y_done = sem("f_out_done"), sem("f_y_done")
        y_stored = [sem("f_y_stored0"), sem("f_y_stored1")]
        AHEAD = 2
        FREE = SUB + START

        block = ctx.enter_context(nc.Block())

        rows = [slice(kt * P, (kt + 1) * P) for kt in range(KT)]
        jobs = [(wo_t[rows[kt], :], wo_hi[:, kt, :], wo_lo[:, kt, :]) for kt in range(KT)]
        jobs += [(router_t[rows[kt], :], r_hi[:, kt, :], r_lo[:, kt, :]) for kt in range(KT)]
        jobs += [(lora_a[rows[kt], :], a_hi[:, kt, :], a_lo[:, kt, :]) for kt in range(KT)]
        jobs += [(base_t[rows[kt], :], base_hi[:, kt, :], base_lo[:, kt, :]) for kt in range(KT)]
        jobs += [(lora_b, b_hi[:, :], b_lo[:, :])]
        weights = Weights(jobs, w_raw, w_loaded, w_hi_done, w_lo_done)

        @block.sync
        def _(sp):
            for u in range(2):
                sp.dma_start(xin[u][:, :, :], x_v[u]).then_inc(x_loaded[u], 16)
            sp.dma_start(bias[:, :], base_b.to_broadcast([P, DM])).then_inc(bias_loaded, 16)
            sp.dma_start(r_bias[:, :], router_b.to_broadcast([P, E])).then_inc(bias_loaded, 16)
            for n in range(W_RING, len(jobs)):
                weights.load(sp, n)

            def load(T, b, n, u):
                sp.wait_ge(c_lo_done, T + START)
                sp.dma_start(cin, ctx_v[b, :, :, n]).then_inc(ctx_loaded, 16)
                if not (isinstance(T, int) and T < 2):
                    sp.wait_ge(y_done, 4 * T + START)
                    sp.dma_start(xin[u][:, :, :], x_v[T]).then_inc(x_loaded[u], 16)

            load(1, 0, slice(TT, 2 * TT), 1)
            for u in range(2):
                load(2 + u, 0, slice((2 + u) * TT, (3 + u) * TT), u)
            with sp.Fori(0, QT // 2) as half:
                for u in range(2):
                    load(QT + 2 * half + u, 1, bass.ds(1024 * half + 512 * u, TT), u)

        @block.gpsimd
        def _(pool):
            for semaphore in (c_lo_done, mid_copied, mid_gated, out_done, *y_stored):
                pool.sem_inc(semaphore, START)
            pool.memset(ident[:, :], 0.0).then_inc(zeroed, 1)
            pool.wait_ge(zeroed, 1)
            pool.memset(lower[:, :, :], 1.0).then_inc(zeroed, 1)
            pool.wait_ge(zeroed, 2)
            pool.affine_select(ident[:, :], ident[:, :], pattern=[[-1, P]], compare_op=ALU.not_equal,
                               fill=1.0, base=0, channel_multiplier=1).then_inc(consts_done, 1)
            pool.affine_select(lower[:, :, :], lower[:, :, :], pattern=[[1, E], [-1, E]], compare_op=ALU.is_gt,
                               fill=0.0, base=0, channel_multiplier=0).then_inc(consts_done, 1)
            pool.wait_ge(bias_loaded, 32)
            with pool.Fori(0, TILES // 2) as i:
                for u in range(2):
                    T = 2 * i + u
                    pool.wait_ge(xn_done, T + 1)
                    for s in range(SUB):
                        ins = pool.tensor_tensor(xin[u][:, s, :], xin[u][:, s, :], bias[:, :], ALU.add)
                    ins.then_inc(biased, 1)

        @block.tensor
        def _(pe):
            def product(out, pairs, done):
                for n, (w, a) in enumerate(pairs):
                    mm = pe.matmul(out, w, a, start=(n == 0), stop=(n == len(pairs) - 1))
                if done is not None:
                    mm.then_inc(done, 1)

            def attention_out(T, u, s):
                m = 4 * T + s
                if s == 0:
                    pe.wait_ge(c_lo_done, T + 1 + START)
                pe.wait_ge(added, m + 1)
                tok = slice(s * P, (s + 1) * P)
                product(wo_ps[s % 2][:, :], [(c[:, u, kt, tok], w[:, kt, :]) for c, w in
                        ((c_hi, wo_hi), (c_hi, wo_lo), (c_lo, wo_hi)) for kt in range(KT)], wo_done)

            def transposes(T, kt):
                if kt == 0:
                    pe.wait_ge(xn_done, T + 1)
                if not (isinstance(T, int) and 4 * T + kt - 1 <= 0):
                    pe.wait_ge(xt_lo_done, 4 * T + kt - 1)
                for s in range(SUB):
                    mm = pe.transpose(tr_ps[kt % 2][:, s * P:(s + 1) * P], xn[:, s, kt * P:(kt + 1) * P], ident[:, :])
                mm.then_inc(tr_done, 1)

            def router(T, u):
                pe.wait_ge(mid_gated, T + START)
                for kt in range(KT):
                    pe.wait_ge(xt_lo_done, 4 * T + kt + 1)
                    for n, (w, a) in enumerate(((r_hi, xt_hi), (r_lo, xt_hi), (r_hi, xt_lo))):
                        mm = pe.matmul(lg_ps[0:E, :], w[:, kt, :], a[:, u, kt, :],
                                       start=(kt == 0 and n == 0), stop=(kt == KT - 1 and n == 2))
                mm.then_inc(router_done, 1)

            def down(T, u):
                pe.wait_ge(mid_copied, T + START)
                product(mid_ps[:, :], [(w[:, kt, :], a[:, u, kt, :]) for w, a in
                        ((a_hi, xt_hi), (a_lo, xt_hi), (a_hi, xt_lo)) for kt in range(KT)], mid_done)

            def turn_logits(T):
                wait_alone(pe, logit_copied, T + 1, pe_passed)
                for s in range(SUB):
                    mm = pe.transpose(lg_ps[:, s * E:(s + 1) * E], logit_t[:, s * P:(s + 1) * P], ident[0:E, 0:E])
                mm.then_inc(logit_turned, 1)

            def base(T, u, s):
                pe.wait_ge(y_done, 4 * T + s - 1 + FREE)
                pairs = [(a[:, u, kt, s * P:(s + 1) * P], w[:, kt, :]) for a, w in
                         ((xt_hi, base_hi), (xt_hi, base_lo), (xt_lo, base_hi)) for kt in range(KT)]
                for n, (w, a) in enumerate(pairs):
                    pe.matmul(out_ps[s % 2][:, :], w, a, start=(n == 0), stop=False)

            def turn_gates(T):
                pe.wait_ge(gated, T + 1)
                for s in range(SUB):
                    mm = pe.transpose(lg_ps[:, s * P:(s + 1) * P], gate_x[:, s, :], ident[:, :])
                mm.then_inc(gate_turned, 1)

            def experts(T, s):
                pe.wait_ge(mt_lo_done, T + 1)
                tok = slice(s * P, (s + 1) * P)
                pairs = ((mt_hi, b_hi), (mt_hi, b_lo), (mt_lo, b_hi))
                for n, (a, w) in enumerate(pairs):
                    mm = pe.matmul(out_ps[s % 2][:, :], a[:, tok], w[:, :], start=False, stop=(n == len(pairs) - 1))
                mm.then_inc(out_done, 1)

            def tile(T, u, more):
                router(T, u)
                down(T, u)
                turn_logits(T)
                if more:
                    attention_out(T + 1, 1 - u, 0)
                    attention_out(T + 1, 1 - u, 1)
                base(T, u, 0)
                base(T, u, 1)
                turn_gates(T)
                if more:
                    attention_out(T + 1, 1 - u, 2)
                experts(T, 0)
                experts(T, 1)
                if more:
                    attention_out(T + 1, 1 - u, 3)
                base(T, u, 2)
                experts(T, 2)
                base(T, u, 3)
                if more:
                    transposes(T + 1, 0)
                    transposes(T + 1, 1)
                experts(T, 3)
                if more:
                    transposes(T + 1, 2)
                    transposes(T + 1, 3)

            pe.wait_ge(consts_done, 2)
            pe.wait_ge(w_lo_done, KT)
            for s in range(SUB):
                attention_out(0, 0, s)
            for kt in range(KT):
                transposes(0, kt)
            pe.wait_ge(w_lo_done, len(jobs))
            with pe.Fori(0, TILES // 2 - 1) as i:
                for u in range(2):
                    tile(2 * i + u, u, True)
            tile(TILES - 2, 0, True)
            tile(TILES - 1, 1, False)

        @block.scalar
        def _(act):
            def ctx_copy(T, u):
                act.wait_ge(ctx_loaded, 16 * T + 16)
                act.activation(c_hi[:, u], cin, ACT.Copy).then_inc(c_hi_done, 1)

            def root(T):
                act.wait_ge(var_done, T + 1)
                act.activation(std[:, :], mv[:, :, 1], ACT.Sqrt, bias=EPS).then_inc(std_done, 1)

            def xt_copy(T, u, kt):
                act.wait_ge(tr_done, 4 * T + kt + 1)
                act.activation(xt_hi[:, u, kt, :], tr_ps[kt % 2][:, :], ACT.Copy).then_inc(xt_hi_done, 1)

            def tile(T, u, more, load):
                act.wait_ge(router_done, T + 1)
                act.activation(logit_t[:, :], lg_ps[0:E, :], ACT.Copy).then_inc(logit_copied, 1)
                act.wait_ge(mid_done, T + 1)
                act.wait_ge(mid_gated, T + START)
                act.activation(mid[:, :], mid_ps[:, :], ACT.Copy).then_inc(mid_copied, 1)
                act.wait_ge(shift_done, T + 1)
                act.activation(ex[:, :, :], shifted[:, :, :], ACT.Exp).then_inc(ex_done, 1)
                act.wait_ge(mid_gated, T + 1 + START)
                act.wait_ge(out_done, 4 * T + START)
                act.activation(mt_hi[:, :], gated_mid[:, :], ACT.Copy).then_inc(mt_hi_done, 1)
                if more:
                    root(T + 1)
                    for kt in range(KT):
                        xt_copy(T + 1, 1 - u, kt)
                if load:
                    act.wait_ge(wo_done, 4 * T + 4)
                    ctx_copy(T + 2, u)
                act.wait_ge(y_done, 4 * T + 4 + FREE)
                act.dma_start(out_v[T], y[:, u]).then_inc(y_stored[u], 16)

            for n in range(3 * KT):
                if n == KT:
                    ctx_copy(0, 0)
                weights.round(act, n)
            root(0)
            for kt in range(KT):
                weights.round(act, 3 * KT + kt)
                xt_copy(0, 0, kt)
            weights.round(act, len(jobs) - 1)
            ctx_copy(1, 1)
            with act.Fori(0, TILES // 2 - 1) as i:
                for u in range(2):
                    tile(2 * i + u, u, True, True)
            tile(TILES - 2, 0, True, False)
            tile(TILES - 1, 1, False, False)
            for u in range(2):
                act.wait_ge(y_stored[u], 16 * TILES // 2 + START)

        @block.vector
        def _(dve):
            LINKS = 14

            def ctx_rest(T, u):
                dve.wait_ge(c_hi_done, T + 1)
                dve.tensor_tensor(c_lo[:, u], cin, c_hi[:, u].bitcast(F32), ALU.subtract).then_inc(c_lo_done, 1)

            def add(T, i, u, s):
                if s == 0:
                    dve.wait_ge(x_loaded[u], 16 * i + 16)
                dve.wait_ge(wo_done, 4 * T + s + 1)
                xs = xin[u][:, s, :]
                dve.tensor_tensor(xs, wo_ps[s % 2][:, :], xs, ALU.add).then_inc(added, 1)
                dve.wait_ge(added, 4 * T + s + 1 + AHEAD)
                dve.bn_stats(stats[:, s, :], xs).then_inc(stats_done, 1)

            def variances(T):
                wait_alone(dve, stats_done, 4 * T + 4, passed)
                for s in range(SUB):
                    ins = dve.bn_aggr(mv[:, s, :], stats[:, s, :])
                ins.then_inc(var_done, 1)

            def normalise(T, u):
                dve.wait_ge(std_done, T + 1)
                dve.reciprocal(rstd[:, :], std[:, :]).then_inc(rstd_done, 1)
                dve.wait_ge(rstd_done, T + 1)
                for s in range(SUB):
                    ins = dve.tensor_scalar(xn[:, s, :], xin[u][:, s, :], mv[:, s, 0:1], rstd[:, s:s + 1],
                                            ALU.subtract, ALU.mult)
                ins.then_inc(xn_done, 1)

            def xt_rest(T, u, kt):
                dve.wait_ge(xt_hi_done, 4 * T + kt + 1)
                dve.tensor_tensor(xt_lo[:, u, kt, :], tr_ps[kt % 2][:, :], xt_hi[:, u, kt, :].bitcast(F32),
                                  ALU.subtract).then_inc(xt_lo_done, 1)

            def gates(T):
                count = [0]

                def after(ins):
                    count[0] += 1
                    ins.then_inc(link, 1)
                    dve.wait_ge(link, LINKS * T + count[0])

                def wide(a):
                    return a[:, :].unsqueeze(2).to_broadcast([P, SUB, E])

                other = prob[:, :, :].unsqueeze(2).to_broadcast([P, SUB, E, E])
                own = prob[:, :, :].unsqueeze(3).to_broadcast([P, SUB, E, E])
                dve.wait_ge(logit_turned, T + 1)
                after(dve.tensor_tensor(logit[:, :, :], lg_ps[:, 0:SUB * E].rearrange("p (s e) -> p s e", e=E),
                                        r_bias[:, :].unsqueeze(1).to_broadcast([P, SUB, E]), ALU.add))
                after(dve.tensor_reduce(top[:, :], logit[:, :, :], AX.X, ALU.max))
                dve.tensor_tensor(shifted[:, :, :], logit[:, :, :], wide(top), ALU.subtract).then_inc(shift_done, 1)
                dve.wait_ge(ex_done, T + 1)
                after(dve.tensor_reduce(den[:, :], ex[:, :, :], AX.X, ALU.add))
                after(dve.reciprocal(rden[:, :], den[:, :]))
                after(dve.tensor_tensor(prob[:, :, :], ex[:, :, :], wide(rden), ALU.mult))
                after(dve.tensor_tensor(above[:, :, :, :], other, own, ALU.is_gt))
                after(dve.tensor_tensor(ties[:, :, :, :], other, own, ALU.is_equal))
                after(dve.tensor_tensor(ties[:, :, :, :], ties[:, :, :, :],
                                        lower[:, :, :].unsqueeze(1).to_broadcast([P, SUB, E, E]), ALU.mult))
                after(dve.tensor_tensor(above[:, :, :, :], above[:, :, :, :], ties[:, :, :, :], ALU.add))
                after(dve.tensor_reduce(rank[:, :, :], above[:, :, :, :], AX.X, ALU.add))
                after(dve.scalar_tensor_tensor(picked[:, :, :], rank[:, :, :], 1.5, prob[:, :, :], ALU.is_lt, ALU.mult))
                after(dve.tensor_reduce(psum2[:, :], picked[:, :, :], AX.X, ALU.add))
                after(dve.reciprocal(rpsum2[:, :], psum2[:, :]))
                after(dve.scalar_tensor_tensor(gate[:, :, :], picked[:, :, :], LORA_SCALING, wide(rpsum2), ALU.mult, ALU.mult))
                assert count[0] == LINKS
                gate_r = gate[:, :, :].rearrange("p s e -> p (s e)").unsqueeze(2).to_broadcast([P, SUB * E, RANK])
                dve.tensor_copy(gate_x[:, :, :].rearrange("p s (e r) -> p (s e) r", r=RANK), gate_r).then_inc(gated, 1)

            def gate_mid(T):
                dve.wait_ge(gate_turned, T + 1)
                dve.wait_ge(mid_copied, T + 1 + START)
                dve.tensor_tensor(gated_mid[:, :], lg_ps[:, :], mid[:, :], ALU.mult).then_inc(mid_gated, 1)

            def mid_rest(T):
                dve.wait_ge(mt_hi_done, T + 1)
                dve.tensor_tensor(mt_lo[:, :], gated_mid[:, :], mt_hi[:, :].bitcast(F32), ALU.subtract).then_inc(mt_lo_done, 1)

            def final(T, i, u, s):
                dve.wait_ge(out_done, 4 * T + s + 1 + START)
                if s == 0:
                    dve.wait_ge(biased, T + 1)
                    dve.wait_ge(y_stored[u], 16 * i + START)
                dve.tensor_tensor(y[:, u, s, :], out_ps[s % 2][:, :], xin[u][:, s, :], ALU.add).then_inc(y_done, 1)

            def tile(T, i, u, more, load):
                gates(T)
                if more:
                    add(T + 1, i + u, 1 - u, 0)
                    add(T + 1, i + u, 1 - u, 1)
                gate_mid(T)
                mid_rest(T)
                if more:
                    add(T + 1, i + u, 1 - u, 2)
                final(T, i, u, 0)
                final(T, i, u, 1)
                if more:
                    add(T + 1, i + u, 1 - u, 3)
                    variances(T + 1)
                    normalise(T + 1, 1 - u)
                    for kt in range(KT):
                        xt_rest(T + 1, 1 - u, kt)
                final(T, i, u, 2)
                final(T, i, u, 3)
                if load:
                    ctx_rest(T + 2, u)

            dve.sem_inc(added, AHEAD)
            dve.sem_inc(y_done, FREE)
            for n in range(KT):
                weights.rest(dve, n)
            ctx_rest(0, 0)
            for n in range(KT, 2 * KT):
                weights.rest(dve, n)
            for s in range(SUB):
                add(0, 0, 0, s)
                weights.rest(dve, 2 * KT + s)
            variances(0)
            normalise(0, 0)
            for kt in range(KT):
                weights.rest(dve, 3 * KT + kt)
                xt_rest(0, 0, kt)
            weights.rest(dve, len(jobs) - 1)
            ctx_rest(1, 1)
            dve.wait_ge(consts_done, 2)
            dve.wait_ge(bias_loaded, 32)
            with dve.Fori(0, TILES // 2 - 1) as i:
                for u in range(2):
                    tile(2 * i + u, i, u, True, True)
            tile(TILES - 2, TILES // 2 - 1, 0, True, False)
            tile(TILES - 1, TILES // 2 - 1, 1, False, False)


def layer(nc, x, wq_t, wk_t, wv_t, wo_t, rope, base_t, base_b, router_t, router_b, lora_a, lora_b, out):
    qk_scr = nc.dram_tensor("qk_scratch", [4, GROUPS, P, SEQ], F32, kind="Internal").ap()
    v_scr = nc.dram_tensor("v_scratch", [GROUPS, SEQ, P], F32, kind="Internal").ap()
    ctx_scr = nc.dram_tensor("ctx_scratch", [GROUPS, P, SEQ], F32, kind="Internal").ap()
    with ExitStack() as ctx:
        shared = ctx.enter_context(nc.sbuf_tensor("shared", [P, W_RING * DM], F32))[:, :]
        early = Early(nc, ctx, shared, ctx_scr, wo_t)
        project(nc, x, wq_t, wk_t, wv_t, rope, qk_scr, v_scr, shared)
        attend(nc, qk_scr, v_scr, ctx_scr, shared, early.loads)
        finish(nc, early, x, wo_t, base_t, base_b, router_t, router_b, lora_a, lora_b, out)


def rope_tables():
    inv = np.exp(np.float32(-np.log(THETA)) * np.arange(0, DK, 2, dtype=np.float32) / np.float32(DK)).astype(np.float32)
    angle = (np.arange(SEQ, dtype=np.float32)[None, :] * inv[:, None]).astype(np.float32).astype(np.float64)
    one = np.stack([-np.sin(angle), np.cos(angle), np.sin(angle)], axis=1).astype(np.float32)
    return np.ascontiguousarray(np.tile(one, (P // (DK // 2), 1, BATCH)))


def kernel(L0_attn_x, L0_attn_Wq, L0_attn_Wk, L0_attn_Wv, L0_attn_Wo, L0_ffn_base_w, L0_ffn_base_b,
           L0_ffn_router_w, L0_ffn_router_b, L0_ffn_lora_A, L0_ffn_lora_B):
    import concourse.bacc as bacc
    from concourse.bass_utils import run_bass_kernel_spmd

    def turned(w):
        return np.ascontiguousarray(np.transpose(np.asarray(w)))

    def halves(w):
        return np.ascontiguousarray(np.asarray(w).reshape(2, 8, DK // 2, 2, DM).transpose(4, 0, 3, 1, 2).reshape(DM, DM))

    arrays = {
        "x": np.asarray(L0_attn_x).reshape(TOKENS, DM),
        "wq_t": halves(L0_attn_Wq),
        "wk_t": halves(L0_attn_Wk),
        "wv_t": turned(L0_attn_Wv),
        "wo_t": turned(L0_attn_Wo),
        "rope": rope_tables(),
        "base_t": turned(L0_ffn_base_w),
        "base_b": np.asarray(L0_ffn_base_b).reshape(1, DM),
        "router_t": turned(L0_ffn_router_w),
        "router_b": np.asarray(L0_ffn_router_b).reshape(1, EXPERTS),
        "lora_a": np.ascontiguousarray(np.asarray(L0_ffn_lora_A).transpose(1, 0, 2).reshape(DM, EXPERTS * RANK)),
        "lora_b": np.asarray(L0_ffn_lora_B).reshape(EXPERTS * RANK, DM),
    }
    nc = bacc.Bacc("TRN2", target_bir_lowering=False, num_devices=1)
    args = [nc.dram_tensor(f"in_{name}", a.shape, F32, kind="ExternalInput").ap() for name, a in arrays.items()]
    out = nc.dram_tensor("out", [TOKENS, DM], F32, kind="ExternalOutput").ap()
    nc.disable_value_cache = True
    layer(nc, *args, out)
    r = run_bass_kernel_spmd(nc, [{f"in_{name}": a for name, a in arrays.items()}], core_ids=[0])
    return r.results[0]["out"].reshape(BATCH, SEQ, DM)
```
